# Optimizing a Trainium2 kernel written in Bass

```python
import numpy as np
import jax
import jax.numpy as jnp

def _softmax(x, axis=-1):
    return jax.nn.softmax(x, axis=axis)

def _gelu(x):
    return jax.nn.gelu(x, approximate=True)

def _silu(x):
    return jax.nn.silu(x)

def _sigmoid(x):
    return jax.nn.sigmoid(x)

def _layernorm(x, axis=-1, eps=1e-05):
    m = jnp.mean(x, axis=axis, keepdims=True)
    v = jnp.var(x, axis=axis, keepdims=True)
    return (x - m) / jnp.sqrt(v + eps)

def _scatter_add(tgt, idx, src, axis=0):
    return tgt.at[idx].add(src)

def _segment_sum(src, seg, n):
    return jax.ops.segment_sum(src, seg, n)
kernel_name = 'mk_seq_postln_d1_jaxref_r8_c23313'

def setup_inputs(seed: int=0):
    np.random.seed(seed)
    _w = jnp.asarray

    def _L0_attn_setup():
        import math
        import jax, jax.numpy as jnp
        import numpy as np
        B, C, D = (4, 256, 128)
        DQ = DV = 64
        H = 16
        key = jax.random.key(seed)
        kx, kq, kk, kv, kw = jax.random.split(key, 5)
        x = jax.random.normal(kx, (B, C, D), dtype=jnp.float32)
        Q = jax.random.normal(kq, (DQ, D, H), dtype=jnp.float32) / math.sqrt(D)
        K = jax.random.normal(kk, (DQ, D, H), dtype=jnp.float32) / math.sqrt(D)
        V = jax.random.normal(kv, (DV, D, H), dtype=jnp.float32) / math.sqrt(D)
        W = jax.random.normal(kw, (D, DV, H), dtype=jnp.float32) / math.sqrt(DV)
        return {'x': x, 'Q': Q, 'K': K, 'V': V, 'W': W}
    _L0_attn_in = _L0_attn_setup()

    def _L0_ffn_setup():
        import jax, jax.numpy as jnp
        import numpy as np
        B, T, C, H, E, K = (4, 128, 128, 512, 8, 2)
        key = jax.random.key(seed)
        ks = jax.random.split(key, 5)
        scale = 0.02
        return {'x': jax.random.normal(ks[0], (B, T, C), dtype=jnp.float32), 'Wg': jax.random.normal(ks[1], (C, E), dtype=jnp.float32) * scale, 'W1': jax.random.normal(ks[2], (E, C, H), dtype=jnp.float32) * scale, 'W3': jax.random.normal(ks[3], (E, C, H), dtype=jnp.float32) * scale, 'W2': jax.random.normal(ks[4], (E, H, C), dtype=jnp.float32) * scale}
    _L0_ffn_in = _L0_ffn_setup()
    _d = {'L0_attn_x': _L0_attn_in['x'], 'L0_attn_Q': _L0_attn_in['Q'], 'L0_attn_K': _L0_attn_in['K'], 'L0_attn_V': _L0_attn_in['V'], 'L0_attn_W': _L0_attn_in['W'], 'L0_ffn_Wg': _L0_ffn_in['Wg'], 'L0_ffn_W1': _L0_ffn_in['W1'], 'L0_ffn_W3': _L0_ffn_in['W3'], 'L0_ffn_W2': _L0_ffn_in['W2']}
    _x0 = _d['L0_attn_x']
    _d['L0_attn_x'] = jax.random.normal(jax.random.fold_in(jax.random.key(seed), 1), (32, 256, 128), dtype=_x0.dtype)
    del _x0
    return _d

def reference(L0_attn_x, L0_attn_Q, L0_attn_K, L0_attn_V, L0_attn_W, L0_ffn_Wg, L0_ffn_W1, L0_ffn_W3, L0_ffn_W2):

    def _L0_attn_ref(x, Q, K, V, W):
        import math
        import jax, jax.numpy as jnp
        import numpy as np
        B, C, D = (4, 256, 128)
        DQ = DV = 64
        H = 16
        d_query, d_embed, num_heads = Q.shape
        d_value = V.shape[0]
        sq = math.sqrt(d_query / d_embed)
        sv = math.sqrt(d_value / d_embed)
        q = jnp.einsum('qdh,bcd->bhcq', Q, x) * sq
        k = jnp.einsum('qdh,bcd->bhcq', K, x) * sq
        v = jnp.einsum('vdh,bcd->bhcv', V, x) * sv
        att = jnp.einsum('bhcq,bhCq->bhcC', q, k) / d_query
        T = x.shape[1]
        causal = jnp.arange(T)[:, None] >= jnp.arange(T)[None, :]
        att = jnp.where(causal, att, -jnp.inf)
        p = jax.nn.softmax(att, axis=-1)
        y = jnp.einsum('bhcC,bhCv->bhcv', p, v)
        z = jnp.einsum('dvh,bhcv->bcd', W, y) * (math.sqrt(d_embed / d_value) / num_heads)
        return z

    def _L0_ffn_ref(x, Wg, W1, W3, W2):
        import jax, jax.numpy as jnp
        import numpy as np
        B, T, C, H, E, K = (4, 128, 128, 512, 8, 2)
        Bb, Tt, Cc = x.shape
        x_flat = x.reshape(-1, Cc)
        logits = x_flat @ Wg
        probs = jax.nn.softmax(logits, axis=-1)
        top_w, top_idx = jax.lax.top_k(probs, K)
        top_w = top_w / jnp.sum(top_w, axis=-1, keepdims=True)
        combine = jnp.sum(jax.nn.one_hot(top_idx, E, dtype=x.dtype) * top_w[..., None], axis=1)
        h1 = jnp.einsum('nc,ech->neh', x_flat, W1)
        h3 = jnp.einsum('nc,ech->neh', x_flat, W3)
        hidden = jax.nn.silu(h1) * h3
        expert_out = jnp.einsum('neh,ehc->nec', hidden, W2)
        out = jnp.einsum('ne,nec->nc', combine, expert_out)
        return out.reshape(Bb, Tt, Cc)
    x = L0_attn_x
    x = _layernorm(x + _L0_attn_ref(x, L0_attn_Q, L0_attn_K, L0_attn_V, L0_attn_W), axis=-1)
    x = _layernorm(x + _L0_ffn_ref(x, L0_ffn_Wg, L0_ffn_W1, L0_ffn_W3, L0_ffn_W2), axis=-1)
    return x

_drawn_inputs = setup_inputs


def setup_inputs(seed=0):
    import zlib

    import numpy as np

    out = dict(_drawn_inputs(seed))
    spreads = {}
    factors = {'L0_attn_Q': 8.0,
     'L0_attn_K': 8.0,
     'L0_ffn_Wg': 7.786,
     'L0_ffn_W1': 6.866,
     'L0_ffn_W3': 6.826,
     'L0_ffn_W2': 6.834}
    for name, (base, spread) in spreads.items():
        noise = np.random.default_rng([zlib.crc32(name.encode()), seed]).standard_normal(out[name].shape)
        drawn = base * np.exp(spread * noise) if base else spread * noise
        out[name] = jnp.asarray(drawn.astype(out[name].dtype))
    for name, factor in factors.items():
        out[name] = (out[name] * factor).astype(out[name].dtype)
    return out
```

```python
from contextlib import ExitStack

import concourse.bass as bass
from concourse import mybir

F32 = mybir.dt.float32
F32R = mybir.dt.float32r
BF16 = mybir.dt.bfloat16
I32 = mybir.dt.int32
U32 = mybir.dt.uint32
ALU = mybir.AluOpType
ACT = mybir.ActivationFunctionType
AX = mybir.AxisListType

P = 128
BIG = 1.0e30
EPS = 1e-05


def wait_alone(eng, met, *waits):
    waits = [(s, c if isinstance(c, int) else eng.to_reg(c)) for s, c in waits]
    eng.wait_ge(met, 1)
    for s, c in waits:
        if not isinstance(c, int) or c > 0:
            eng.wait_ge(s, c)


def attention_phase(nc, ctx, keep, xT, x, wq, wk, wv, wz, wg, w1, w3, w2, x1_dram, slot_list):
    NB, C, D = x.shape
    N = NB * C
    E = wg.shape[1]
    F = w1.shape[2]
    GROUPS = 2 * (C // P) * 2
    H, HD = 16, 64
    NP = H // 2
    TC = C // P
    TRIPS = NB // 2
    SCALE = 1.0 / P
    RAW = 8
    REGION = N

    def sb(name, shape, dt=F32):
        return ctx.enter_context(nc.sbuf_tensor(name, shape, dt))

    def sem(name):
        return ctx.enter_context(nc.semaphore(name))

    w_raw = sb("w_raw", [P, 4, H * HD])
    wq_hi, wq_lo = sb("wq_hi", [P, H * HD], F32R), sb("wq_lo", [P, H * HD], F32R)
    wk_hi, wk_lo = sb("wk_hi", [P, H * HD], F32R), sb("wk_lo", [P, H * HD], F32R)
    wv_hi, wv_lo = sb("wv_hi", [P, H * HD], F32R), sb("wv_lo", [P, H * HD], F32R)
    wz_s = sb("wz_s", [P, NP, D])
    xT_raw = [sb(f"xT_raw{i}", [P, C]) for i in range(2)]
    xT_hi = [sb(f"xT_hi{i}", [P, C], F32R) for i in range(2)]
    xT_lo = [sb(f"xT_lo{i}", [P, C], F32R) for i in range(2)]
    x_res = [sb(f"x_res{i}", [P, TC, D]) for i in range(2)]
    qk_hi = [sb(f"qk_hi{i}", [P, 2 * C], F32R) for i in range(2)]
    qk_lo = [sb(f"qk_lo{i}", [P, 2 * C], F32R) for i in range(2)]
    nmax = [sb(f"nmax{i}", [P, 2, 2]) for i in range(2)]
    p_sb = [sb(f"p_sb{i}", [P, 2, 384]) for i in range(2)]
    pT_sb = [sb(f"pT_sb{i}", [P, 2, 384]) for i in range(2)]
    v_sb = [sb(f"v_sb{i}", [P, TC, H, HD + 1]) for i in range(2)]
    rinv = [sb(f"rinv{i}", [P, TC, 2]) for i in range(2)]
    yn = [sb(f"yn{i}", [P, TC, 2, HD]) for i in range(2)]
    yT_sb = [sb(f"yT_sb{i}", [P, C]) for i in range(2)]
    zT_sb = sb("zT_sb", [P, C])
    r_sb = [sb(f"r_sb{i}", [P, TC, D]) for i in range(2)]
    stats = [sb(f"stats{i}", [P, TC, 6]) for i in range(2)]
    mv = [sb(f"mv{i}", [P, TC, 2]) for i in range(2)]
    veps = [sb(f"veps{i}", [P, TC]) for i in range(2)]
    rstd = [sb(f"rstd{i}", [P, TC]) for i in range(2)]
    x1_cur = [sb(f"x1_cur{i}", [P, TC, D]) for i in range(2)]
    x1T_sb = sb("x1T_sb", [P, C])
    wg_sb = sb("wg_sb", [P, E])
    lg = sb("lg", [P, GROUPS // 2, E])
    top = sb("top", [P, 2, GROUPS // 2])
    eq = sb("eq", [P, GROUPS // 2, E])
    rank = sb("rank", [P, GROUPS // 2])
    lg2 = sb("lg2", [P, GROUPS // 2, E])
    desc = sb("desc", [P, GROUPS // 2, E])
    desc_i = sb("desc_i", [P, GROUPS // 2, E], I32)
    onehot = sb("onehot", [P, GROUPS // 2, 2, E])
    onehot_b = sb("onehot_b", [P, GROUPS // 2, 2, E], BF16)
    gap = sb("gap", [P, GROUPS // 2])
    egap = sb("egap", [P, GROUPS // 2])
    egap1 = sb("egap1", [P, GROUPS // 2])
    place = sb("place", [P, GROUPS, E])
    slot_f = sb("slot_f", [P, GROUPS])
    slot_u = sb("slot_u", [P, GROUPS], U32)
    entry = sb("entry", [P, GROUPS, 3], U32)
    entry_step = sb("entry_step", [P, GROUPS, 2], U32)
    blank = sb("blank", [P, slot_list.shape[0] // P, 3], U32)
    region_i = sb("region_i", [P, E], I32)
    tri = sb("tri", [P, P], BF16)
    ones_b = sb("ones_b", [P, P], BF16)
    x1_cen = [sb(f"x1_cen{i}", [P, TC, D]) for i in range(2)]
    neghalf = sb("neghalf", [P, TC])
    eps = sb("eps", [P, TC])
    ident = sb("ident", [P, P])
    ident_b = sb("ident_b", [P, P], BF16)
    mask = sb("mask", [P, 2, P], BF16)

    S = [ctx.enter_context(nc.psum_tensor(f"psS{i}", [P, 2, 512], F32)) for i in range(2)]
    QK = ctx.enter_context(nc.psum_tensor("psQK", [P, 512], F32))
    Y = ctx.enter_context(nc.psum_tensor("psY", [P, 512], F32))
    Z = ctx.enter_context(nc.psum_tensor("psZ", [P, 512], F32))
    M = ctx.enter_context(nc.psum_tensor("psM", [P, 512], F32))

    w_landed = sem("w_landed")
    w_hi_done = sem("w_hi_done")
    w_ready = sem("w_ready")
    consts = sem("consts")
    xt_landed = [sem(f"xt_landed{i}") for i in range(2)]
    xr_landed = [sem(f"xr_landed{i}") for i in range(2)]
    xt_hi_done = sem("xt_hi_done")
    xt_split = sem("xt_split")
    qk_done = sem("qk_done")
    qk_hi_done = sem("qk_hi_done")
    qk_split = sem("qk_split")
    scores_done = sem("scores_done")
    max_done = sem("max_done")
    p_ready = sem("p_ready")
    pT_done = sem("pT_done")
    pT_evac = sem("pT_evac")
    y_done = sem("y_done")
    rinv_done = sem("rinv_done")
    y_norm = sem("y_norm")
    yT_done = sem("yT_done")
    yT_evac = sem("yT_evac")
    z_step = sem("z_step")
    z_evac = sem("z_evac")
    v_done = sem("v_done")
    v_evac = sem("v_evac")
    zb_done = sem("zb_done")
    r_ready = sem("r_ready")
    bn_done = sem("bn_done")
    stats_done = sem("stats_done")
    veps_done = sem("veps_done")
    rstd_done = sem("rstd_done")
    cen_done = sem("cen_done")
    x1_ready = sem("x1_ready")
    x1T_done = sem("x1T_done")
    x1T_evac = sem("x1T_evac")
    logits_done = sem("logits_done")
    lg_ready = sem("lg_ready")
    wg_landed = sem("wg_landed")
    route_step = sem("route_step")
    onehot_ready = sem("onehot_ready")
    gap_ready = sem("gap_ready")
    egap_ready = sem("egap_ready")
    prefix_done = sem("prefix_done")
    place_ready = sem("place_ready")
    entry_ready = sem("entry_ready")
    scattered = sem("scattered")
    entry_next = sem("entry_next")
    blank_ready = sem("blank_ready")
    blank_stored = sem("blank_stored")
    route_init = sem("route_init")
    f_landed = [sem(f"f_landed{i}") for i in range(RAW)]
    f_hi_done = sem("f_hi_done")
    f_ready = sem("f_ready")
    x1_stored = [sem(f"x1_stored{i}") for i in range(2)]

    block = ctx.enter_context(nc.Block())

    def wait(eng, s, count):
        if not isinstance(count, int) or count > 0:
            eng.wait_ge(s, count)

    w_hi, w_lo, count = keep["w_hi"], keep["w_lo"], keep["count"]
    pieces = [(m, e) for m in range(3) for e in range(E)]

    def raw_piece(n):
        n %= RAW
        return w_raw[:, n // 2, (n % 2) * F:(n % 2 + 1) * F]

    class At:

        def __init__(self, i, k, first, last):
            self.i, self.k, self.first, self.last = i, k, first, last
            self.kb, self.hp = k // NP, k % NP

        def pair(self, off):
            return self.i * (2 * NP) + (self.k + off)

        def has(self, off):
            return (not self.first or self.k + off >= 0) and (not self.last or self.k + off < 2 * NP)

        def batch(self, off):
            return self.i * 2 + (self.kb + off)

        def has_batch(self, off):
            return (not self.first or self.kb + off >= 0) and (not self.last or self.kb + off < 2)

        def has_route(self, hp):
            return self.k % (2 * NP) == {7: 7, 2: NP + 2, 3: NP + 3}[hp] and not (self.first and self.k < 2 * NP)

        def trip(self):
            return self.i + (self.k // (2 * NP) - 1)

        def hp_of(self, off):
            return (self.k + off) % NP

        def par(self, off):
            return (self.k + off) % 2

        def bpar(self, off):
            return (self.kb + off) % 2

    def trips(eng, step, tail):
        for k in range(2 * NP):
            step(At(0, k, True, False))
        with eng.Fori(1, TRIPS - 1) as i:
            for k in range(2 * NP):
                step(At(i, k, False, False))
        for k in range(2 * NP + tail):
            step(At(TRIPS - 1, k, False, True))

    DRAIN = NP + 4

    @block.sync
    def _(sp):
        for n, w in enumerate((wq, wk, wv)):
            sp.dma_start(w_raw[:, n], w).then_inc(w_landed, 16)
        sp.dma_start(w_raw[:, 3].rearrange("p (n d) -> p n d", d=D), wz.rearrange("(n p) d -> p n d", p=P)).then_inc(w_landed, 16)

        def load_xT(b, j):
            sp.dma_start(xT_raw[j][:], xT[bass.ds(b, 1)].rearrange("b p c -> p (b c)")).then_inc(xt_landed[j], 16)

        def load_x(b, j):
            sp.dma_start(x_res[j][:], x[bass.ds(b, 1)].rearrange("b (t p) d -> p (b t) d", p=P)).then_inc(xr_landed[j], 16)

        def step(at):
            if at.hp != 0:
                return
            if at.has_batch(1):
                wait(sp, xt_split, at.batch(0))
                load_xT(at.batch(1), at.bpar(1))
            if at.has_batch(-1):
                wait(sp, x1_ready, at.batch(0))
                sp.dma_start(x1_dram[bass.ds(at.batch(-1), 1)].rearrange("b (t p) d -> p (b t) d", p=P),
                             x1_cur[at.bpar(-1)][:]).then_inc(x1_stored[at.bpar(-1)], 16)
            if at.has_batch(1):
                wait(sp, r_ready, at.batch(0))
                load_x(at.batch(1), at.bpar(1))

        load_xT(0, 0)
        load_x(0, 0)
        sp.dma_start(wg_sb[:], wg).then_inc(wg_landed, 16)
        trips(sp, step, 1 + NP)
        for j in range(2):
            sp.wait_ge(x1_stored[j], 16 * TRIPS)

    @block.gpsimd
    def _(pool):
        nc.gpsimd.memset(ident[:], 0.0).then_inc(consts, 1)
        nc.gpsimd.memset(ident_b[:], 0.0).then_inc(consts, 1)
        nc.gpsimd.memset(mask[:], 0.0).then_inc(consts, 1)
        nc.gpsimd.memset(tri[:], 1.0).then_inc(consts, 1)
        nc.gpsimd.memset(ones_b[:], 1.0).then_inc(consts, 1)
        nc.gpsimd.memset(neghalf[:], -0.5).then_inc(consts, 1)
        nc.gpsimd.memset(eps[:], EPS).then_inc(consts, 1)
        for j in range(2):
            nc.gpsimd.memset(v_sb[j][:, :, :, HD:HD + 1], 1.0).then_inc(consts, 1)
        pool.wait_ge(consts, 9)
        for m in (ident, ident_b):
            nc.gpsimd.affine_select(out=m[:], in_=m[:], compare_op=ALU.not_equal, fill=1.0, base=0,
                                    pattern=[[-1, P]], channel_multiplier=1).then_inc(consts, 1)
        nc.gpsimd.affine_select(out=mask[:], in_=mask[:], compare_op=ALU.is_ge, fill=BIG, base=0,
                                pattern=[[0, 2], [-1, P]], channel_multiplier=1).then_inc(consts, 1)

        nc.gpsimd.affine_select(out=tri[:], in_=tri[:], compare_op=ALU.is_gt, fill=0.0, base=0,
                                pattern=[[1, P]], channel_multiplier=-1).then_inc(consts, 1)
        rows = slot_list.shape[0] // P
        nc.gpsimd.memset(blank[:], 0).then_inc(blank_ready, 1)
        pool.wait_ge(blank_ready, 1)
        nc.gpsimd.iota(blank[:, :, 1], pattern=[[1, rows]], base=2 * N, channel_multiplier=rows).then_inc(blank_ready, 1)
        pool.wait_ge(blank_ready, 2)
        pool.dma_start(slot_list.rearrange("(p r) w -> p r w", r=rows), blank[:]).then_inc(blank_stored, 16)
        nc.gpsimd.iota(entry[:, :, 0], pattern=[[P, GROUPS // 2], [0, 2]], base=0, channel_multiplier=1).then_inc(route_init, 1)
        nc.gpsimd.iota(entry[:, :, 1], pattern=[[P, GROUPS // 2], [N, 2]], base=0, channel_multiplier=1).then_inc(route_init, 1)
        nc.gpsimd.iota(entry_step[:], pattern=[[0, GROUPS * 2]], base=P * GROUPS // 2, channel_multiplier=0).then_inc(route_init, 1)
        nc.gpsimd.iota(desc_i[:], pattern=[[0, GROUPS // 2], [-1, E]], base=E, channel_multiplier=0).then_inc(route_init, 1)
        nc.gpsimd.iota(region_i[:], pattern=[[REGION, E]], base=0, channel_multiplier=0).then_inc(route_init, 1)

        def load_piece(n):
            m, e = pieces[n]
            src = (w1[e], w3[e], w2[e].rearrange("(a p) c -> p a c", p=P))[m]
            dst = raw_piece(n)
            if m == 2:
                dst = dst.rearrange("p (a c) -> p a c", c=D)
            pool.dma_start(dst, src).then_inc(f_landed[n % RAW], 16)

        def split_piece(n):
            m, e = pieces[n]
            pool.wait_ge(f_hi_done, n + 1)
            nc.gpsimd.tensor_tensor(w_lo[m][:, e], raw_piece(n), w_hi[m][:, e].bitcast(F32), ALU.subtract).then_inc(f_ready, 1)
            if n + RAW < len(pieces):
                pool.wait_ge(f_ready, n + 1)
                load_piece(n + RAW)

        def scatter(t):
            wait_alone(pool, consts, (entry_ready, t + 1))
            for g in range(GROUPS):
                if g:
                    wait_alone(pool, consts, (scattered, (t * GROUPS + g) * 16))
                nc.gpsimd.indirect_dma_start(out=slot_list, out_offset=bass.IndirectOffsetOnAxis(ap=slot_u[:, g:g + 1], axis=0),
                                             in_=entry[:, g], in_offset=None).then_inc(scattered, 16)
            pool.wait_ge(scattered, (t + 1) * (GROUPS * 16))
            nc.gpsimd.tensor_tensor(entry[:, :, 0:2], entry[:, :, 0:2], entry_step[:], ALU.add).then_inc(entry_next, 1)

        def split(b, j, n_trip):
            pool.wait_ge(xt_landed[j], n_trip)
            wait(pool, qk_done, (b - 1) * NP)
            wait(pool, v_done, (b - 1) * 4)
            pool.wait_ge(xt_hi_done, b + 1)
            nc.gpsimd.tensor_tensor(xT_lo[j][:], xT_raw[j][:], xT_hi[j][:].bitcast(F32), ALU.subtract).then_inc(xt_split, 1)

        def step(at):
            if at.first and 2 * at.k < len(pieces):
                for n in (2 * at.k, 2 * at.k + 1):
                    split_piece(n)
            if at.has_route(3):
                scatter(at.trip())
            if at.hp != 0:
                return
            if at.has_batch(1):
                split(at.batch(1), at.bpar(1), (at.i + (at.kb + 1) // 2) * 16 + 16)
            if at.has_batch(-1):
                j = at.bpar(-1)
                b = at.batch(-1)
                wait(pool, stats_done, b + 1)
                if not (at.first and at.kb < 3):
                    wait(pool, x1_stored[j], at.i * 16 + ((at.kb - 1) // 2) * 16)
                nc.gpsimd.tensor_tensor(veps[j][:], mv[j][:, :, 1], eps[:], ALU.add).then_inc(veps_done, 1)
                pool.wait_ge(veps_done, b + 1)
                nc.gpsimd.tensor_tensor(rstd[j][:], veps[j][:], neghalf[:], ALU.pow).then_inc(rstd_done, 1)
                pool.wait_ge(rstd_done, b + 1)
                nc.gpsimd.tensor_tensor(x1_cen[j][:], r_sb[j][:], mv[j][:, :, 0:1].to_broadcast([P, TC, D]),
                                        ALU.subtract).then_inc(cen_done, 1)
                pool.wait_ge(cen_done, b + 1)
                nc.gpsimd.tensor_tensor(x1_cur[j][:], x1_cen[j][:], rstd[j][:].unsqueeze(2).to_broadcast([P, TC, D]),
                                        ALU.mult).then_inc(x1_ready, 1)

        split(0, 0, 16)
        pool.wait_ge(w_ready, 4)
        for n in range(RAW):
            load_piece(n)
        pool.wait_ge(blank_stored, 16)
        trips(pool, step, DRAIN)

    @block.scalar
    def _(act):
        act.wait_ge(w_landed, 64)
        for n, (hi, s) in enumerate(((wq_hi, -SCALE), (wk_hi, 1.0), (wv_hi, 1.0))):
            nc.scalar.activation(hi[:], w_raw[:, n], ACT.Copy, scale=s).then_inc(w_hi_done, 1)
        nc.scalar.activation(wz_s[:].rearrange("p n d -> p (n d)"), w_raw[:, 3], ACT.Copy, scale=1.0 / H).then_inc(w_ready, 1)

        def qk_high(at, off):
            n = at.pair(off)
            j = at.par(off)
            act.wait_ge(qk_done, n + 1)
            wait(act, scores_done, n - 1)
            nc.scalar.activation(qk_hi[j][:], QK[:], ACT.Copy).then_inc(qk_hi_done, 1)

        def xt_high(b, j, n_trip):
            act.wait_ge(xt_landed[j], n_trip)
            wait(act, qk_done, (b - 1) * NP)
            wait(act, v_done, (b - 1) * 4)
            nc.scalar.activation(xT_hi[j][:], xT_raw[j][:], ACT.Copy).then_inc(xt_hi_done, 1)

        def v_copy(b, j, c):
            act.wait_ge(v_done, b * 4 + c + 1)
            if c == 0:
                wait(act, y_done, (b - 1) * NP)
            t, half = c // 2, c % 2
            nc.scalar.activation(v_sb[j][:, t, half * 8:half * 8 + 8, 0:HD],
                                 M[:].rearrange("p (h v) -> p h v", v=HD), ACT.Copy).then_inc(v_evac, 1)

        def step(at):
            if at.has(-3):
                n = at.pair(-3)
                act.wait_ge(yT_done, n + 1)
                wait(act, z_step, n - 1)
                nc.scalar.activation(yT_sb[at.par(-3)][:], Y[:, 0:C], ACT.Copy).then_inc(yT_evac, 1)
            if at.has(1):
                qk_high(at, 1)
            if at.has(0):
                n = at.pair(0)
                j = at.par(0)
                act.wait_ge(max_done, n + 1)
                wait(act, pT_done, n - 1)
                for h in range(2):
                    nc.scalar.activation(p_sb[j][:, h, 0:256], S[j][:, h, 0:256], ACT.Exp, bias=nmax[j][:, h, 0:1], scale=-1.0)
                    last = nc.scalar.activation(p_sb[j][:, h, 256:384], S[j][:, h, 256:384], ACT.Exp,
                                                bias=nmax[j][:, h, 1:2], scale=-1.0)
                last.then_inc(p_ready, 1)
            if at.hp == 2 and at.has_batch(1):
                xt_high(at.batch(1), at.bpar(1), (at.i + (at.kb + 1) // 2) * 16 + 16)
            if at.hp == 0 and at.has_batch(0):
                v_copy(at.batch(0), at.bpar(0), 2)
            if at.hp == 1 and at.has_batch(0):
                v_copy(at.batch(0), at.bpar(0), 3)
            if at.hp == 2 and at.has_batch(-1):
                act.wait_ge(z_step, at.batch(0) * NP)
                wait(act, zb_done, at.batch(-1))
                nc.scalar.activation(zT_sb[:], Z[:, 0:C], ACT.Copy).then_inc(z_evac, 1)
            if at.first and 2 * at.k < len(pieces):
                for n in (2 * at.k, 2 * at.k + 1):
                    m, e = pieces[n]
                    act.wait_ge(f_landed[n % RAW], n // RAW * 16 + 16)
                    nc.scalar.activation(w_hi[m][:, e], raw_piece(n), ACT.Copy).then_inc(f_hi_done, 1)
            if at.hp == 4 and at.has_batch(1):
                v_copy(at.batch(1), at.bpar(1), 0)
            if at.hp == 5 and at.has_batch(-1):
                act.wait_ge(x1T_done, at.batch(0))
                wait(act, logits_done, at.batch(-1))
                nc.scalar.activation(x1T_sb[:], M[:, 0:C], ACT.Copy).then_inc(x1T_evac, 1)
            if at.has_route(7):
                act.wait_ge(gap_ready, at.trip() + 1)
                wait(act, entry_ready, at.trip())
                nc.scalar.activation(egap[:], gap[:], ACT.Exp).then_inc(egap_ready, 1)
            if at.hp == 7 and at.has_batch(1):
                v_copy(at.batch(1), at.bpar(1), 1)

        xt_high(0, 0, 16)
        qk_high(At(0, 0, True, False), 0)
        v_copy(0, 0, 0)
        v_copy(0, 0, 1)
        trips(act, step, DRAIN)

    @block.vector
    def _(dve):
        for n, (hi, lo, s) in enumerate(((wq_hi, wq_lo, -SCALE), (wk_hi, wk_lo, 1.0), (wv_hi, wv_lo, 1.0))):
            dve.wait_ge(w_hi_done, n + 1)
            nc.vector.scalar_tensor_tensor(out=lo[:], in0=w_raw[:, n], scalar=s, in1=hi[:].bitcast(F32),
                                           op0=ALU.mult, op1=ALU.subtract).then_inc(w_ready, 1)

        def qk_low(at, off):
            n = at.pair(off)
            j = at.par(off)
            dve.wait_ge(qk_hi_done, n + 1)
            nc.vector.tensor_tensor(qk_lo[j][:], QK[:], qk_hi[j][:].bitcast(F32), ALU.subtract).then_inc(qk_split, 1)

        def step(at):
            if at.has(0):
                n = at.pair(0)
                j = at.par(0)
                dve.wait_ge(scores_done, n + 1)
                wait(dve, p_ready, n - 1)
                nc.vector.tensor_reduce(nmax[j][:, :, 0], S[j][:, :, 0:256], AX.X, ALU.min)
                nc.vector.tensor_reduce(nmax[j][:, :, 1], S[j][:, :, 256:384], AX.X, ALU.min).then_inc(max_done, 1)
            if at.has(1):
                qk_low(at, 1)
            if at.has(-1):
                n = at.pair(-1)
                j = at.par(-1)
                dve.wait_ge(pT_done, n + 1)
                wait(dve, y_done, n - 1)
                nc.vector.tensor_copy(pT_sb[j][:], S[j][:, :, 0:384]).then_inc(pT_evac, 1)
            if at.has(-2):
                n = at.pair(-2)
                j = at.par(-2)
                y = Y[:, 0:TC * 2 * (HD + 1)].rearrange("p (t h v) -> p t h v", t=TC, v=HD + 1)
                dve.wait_ge(y_done, n + 1)
                nc.vector.reciprocal(rinv[j][:], y[:, :, :, HD]).then_inc(rinv_done, 1)
                dve.wait_ge(rinv_done, n + 1)
                wait(dve, yT_done, n - 1)
                nc.vector.tensor_tensor(yn[j][:], y[:, :, :, 0:HD], rinv[j][:].unsqueeze(3).to_broadcast([P, TC, 2, HD]),
                                        ALU.mult).then_inc(y_norm, 1)
            if at.hp == 3 and at.has_batch(-1):
                b, j = at.batch(-1), at.bpar(-1)
                dve.wait_ge(zb_done, b + 1)
                dve.wait_ge(xr_landed[j], (at.i + (at.kb - 1) // 2) * 16 + 16)
                wait(dve, x1_ready, b - 1)
                nc.vector.tensor_tensor(r_sb[j][:], M[:, 0:TC * D].rearrange("p (t d) -> p t d", t=TC), x_res[j][:],
                                        ALU.add).then_inc(r_ready, 1)
                dve.wait_ge(r_ready, b + 1)
                for t in range(TC):
                    last = nc.vector.bn_stats(stats[j][:, t], r_sb[j][:, t])
                last.then_inc(bn_done, 1)
                wait_alone(dve, consts, (bn_done, b + 1))
                for t in range(TC):
                    last = nc.vector.bn_aggr(mv[j][:, t], stats[j][:, t])
                last.then_inc(stats_done, 1)

            if at.hp == 6 and at.has_batch(-1):
                jt = at.bpar(-1) * TC
                dve.wait_ge(logits_done, at.batch(0))
                nc.vector.tensor_copy(lg[:, jt:jt + TC], M[:, 0:TC * E].rearrange("p (t e) -> p t e", e=E)).then_inc(lg_ready, 1)
            if at.has_route(7):
                choose(at.trip())
            if at.has_route(2):
                assign(at.trip())

        T4 = GROUPS // 2
        STEPS = 16

        def choose(t):
            n = [0]

            def link(ins):
                n[0] += 1
                ins.then_inc(route_step, 1)
                dve.wait_ge(route_step, t * STEPS + n[0])

            def first_of(values, c):
                link(nc.vector.tensor_reduce(top[:, c], values[:], AX.X, ALU.max))
                link(nc.vector.tensor_tensor(eq[:], values[:], top[:, c].unsqueeze(2).to_broadcast([P, T4, E]), ALU.is_equal))
                link(nc.vector.tensor_tensor(lg2[:] if c else eq[:], eq[:], desc[:], ALU.mult))
                link(nc.vector.tensor_reduce(rank[:], (lg2 if c else eq)[:], AX.X, ALU.max))
                link(nc.vector.tensor_tensor(onehot[:, :, c], (lg2 if c else eq)[:],
                                             rank[:].unsqueeze(2).to_broadcast([P, T4, E]), ALU.is_equal))

            dve.wait_ge(lg_ready, t * 2 + 2)
            wait(dve, place_ready, t)
            first_of(lg, 0)
            link(nc.vector.scalar_tensor_tensor(out=lg2[:], in0=onehot[:, :, 0], scalar=-BIG, in1=lg[:], op0=ALU.mult, op1=ALU.add))
            first_of(lg2, 1)
            nc.vector.tensor_copy(onehot_b[:], onehot[:]).then_inc(onehot_ready, 1)
            wait(dve, egap_ready, t)
            nc.vector.tensor_tensor(gap[:], top[:, 1], top[:, 0], ALU.subtract).then_inc(gap_ready, 1)
            assert n[0] == 11

        def assign(t):
            n = [11]

            def link(ins):
                n[0] += 1
                ins.then_inc(route_step, 1)
                dve.wait_ge(route_step, t * STEPS + n[0])

            counts = M[:, 0:(GROUPS + 1) * E].rearrange("p (g e) -> p g e", e=E)
            dve.wait_ge(prefix_done, t + 1)
            wait(dve, entry_next, t)
            link(nc.vector.tensor_tensor(place[:], counts[:, 0:GROUPS], count[:].unsqueeze(1).to_broadcast([P, GROUPS, E]), ALU.add))
            link(nc.vector.tensor_tensor(place[:], place[:], onehot[:].rearrange("p t c e -> p (t c) e"), ALU.mult))
            nc.vector.tensor_tensor(count[:], count[:], counts[:, GROUPS], ALU.add).then_inc(place_ready, 1)
            link(nc.vector.tensor_reduce(slot_f[:], place[:], AX.X, ALU.add))
            nc.vector.tensor_copy(slot_u[:], slot_f[:])
            dve.wait_ge(egap_ready, t + 1)
            link(nc.vector.tensor_scalar(egap1[:], egap[:], 1.0, None, ALU.add))
            w = entry[:].rearrange("p (t c) w -> p t c w", c=2)[:, :, :, 2].bitcast(F32)
            link(nc.vector.reciprocal(w[:, :, 0], egap1[:]))
            nc.vector.tensor_tensor(w[:, :, 1], w[:, :, 0], egap[:], ALU.mult).then_inc(entry_ready, 1)
            assert n[0] == STEPS

        dve.wait_ge(route_init, 5)
        nc.vector.tensor_copy(desc[:], desc_i[:]).then_inc(route_init, 1)
        nc.vector.tensor_copy(count[:], region_i[:]).then_inc(route_init, 1)
        qk_low(At(0, 0, True, False), 0)
        dve.wait_ge(route_init, 7)
        trips(dve, step, DRAIN)

    @block.tensor
    def _(pe):
        def project(at, off):
            n = at.pair(off)
            cols = slice(at.hp_of(off) * P, at.hp_of(off) * P + P)
            b_off = (at.k + off) // NP - at.kb
            if at.hp_of(off) == 0:
                pe.wait_ge(xt_split, at.batch(b_off) + 1)
            wait(pe, qk_split, n)
            j = at.bpar(b_off)
            for o, hi, lo in ((0, wq_hi, wq_lo), (C, wk_hi, wk_lo)):
                out = QK[:, o:o + C]
                nc.tensor.matmul(out, hi[:, cols], xT_hi[j][:], start=True, stop=False)
                nc.tensor.matmul(out, lo[:, cols], xT_hi[j][:], start=False, stop=False)
                last = nc.tensor.matmul(out, hi[:, cols], xT_lo[j][:], start=False, stop=True)
            last.then_inc(qk_done, 1)

        def scores(at):
            n = at.pair(0)
            j = at.par(0)
            wait(pe, pT_evac, n - 1)
            for h in range(2):
                nc.tensor.matmul(S[j][:, h, 128:384], ident_b[:], mask[:].rearrange("p a c -> p (a c)"),
                                 start=True, stop=False, skip_group_check=True)
            pe.wait_ge(qk_split, n + 1)
            for a, (q, k) in enumerate(((qk_hi, qk_hi), (qk_lo, qk_hi), (qk_hi, qk_lo))):
                for o, q0, nk in ((0, P, 2 * P), (2 * P, 0, P)):
                    for h in range(2):
                        r = slice(h * HD, h * HD + HD)
                        last = nc.tensor.matmul(S[j][:, h, o:o + nk], q[j][r, q0:q0 + P], k[j][r, C:C + nk],
                                                start=False, stop=(a == 2), skip_group_check=True)
            last.then_inc(scores_done, 1)

        def transpose_p(at, off):
            n = at.pair(off)
            j = at.par(off)
            pe.wait_ge(p_ready, n + 1)
            for h in range(2):
                for c in range(3):
                    last = nc.tensor.transpose(S[j][:, h, c * P:c * P + P], p_sb[j][:, h, c * P:c * P + P], ident[:])
            last.then_inc(pT_done, 1)

        def values(at, off):
            n = at.pair(off)
            j = at.par(off)
            hp = at.hp_of(off)
            b_off = (at.k + off) // NP - at.kb
            jb = at.bpar(b_off)
            if hp == 0:
                pe.wait_ge(v_evac, at.batch(b_off) * 4 + 4)
            pe.wait_ge(pT_evac, n + 1)
            wait(pe, yT_evac, n)
            for t in range(TC):
                for h in range(2):
                    o = Y[:, (t * 2 + h) * (HD + 1):(t * 2 + h + 1) * (HD + 1)]
                    if t == 0:
                        last = nc.tensor.matmul(o, pT_sb[j][:, h, 256:384], v_sb[jb][:, 0, 2 * hp + h, :], start=True, stop=True)
                    else:
                        nc.tensor.matmul(o, pT_sb[j][:, h, 0:128], v_sb[jb][:, 0, 2 * hp + h, :], start=True, stop=False)
                        last = nc.tensor.matmul(o, pT_sb[j][:, h, 128:256], v_sb[jb][:, 1, 2 * hp + h, :], start=False, stop=True)
            last.then_inc(y_done, 1)

        def transpose_y(at, off):
            n = at.pair(off)
            j = at.par(off)
            pe.wait_ge(y_norm, n + 1)
            for t in range(TC):
                last = nc.tensor.transpose(Y[:, t * P:t * P + P], yn[j][:, t].rearrange("p h v -> p (h v)"), ident[:])
            last.then_inc(yT_done, 1)

        def output(at, off):
            n = at.pair(off)
            hp = at.hp_of(off)
            pe.wait_ge(yT_evac, n + 1)
            if hp == 0:
                b_off = (at.k + off) // NP - at.kb
                wait(pe, z_evac, at.batch(b_off))
            nc.tensor.matmul(Z[:, 0:C], wz_s[:, hp], yT_sb[at.par(off)][:], start=(hp == 0), stop=(hp == NP - 1)).then_inc(z_step, 1)

        def v_chunk(b, j, c, free_sem, free_count):
            wait(pe, free_sem, free_count)
            pe.wait_ge(xt_split, b + 1)
            t, half = c // 2, c % 2
            cols = slice(half * 512, half * 512 + 512)
            rows = slice(t * P, t * P + P)
            nc.tensor.matmul(M[:], xT_hi[j][:, rows], wv_hi[:, cols], start=True, stop=False)
            nc.tensor.matmul(M[:], xT_lo[j][:, rows], wv_hi[:, cols], start=False, stop=False)
            nc.tensor.matmul(M[:], xT_hi[j][:, rows], wv_lo[:, cols], start=False, stop=True).then_inc(v_done, 1)

        def step(at):
            if at.has(0):
                scores(at)
            if at.has(-3):
                transpose_y(at, -3)
            if at.has(1):
                project(at, 1)
            if at.has(-2):
                values(at, -2)
            if at.has(-1):
                transpose_p(at, -1)
            if at.has(-3):
                output(at, -3)
            b, hp = at.batch(0), at.hp
            if hp == 0 and at.has_batch(0):
                v_chunk(b, at.bpar(0), 2, v_evac, b * 4 + 2)
            if hp == 1 and at.has_batch(0):
                v_chunk(b, at.bpar(0), 3, v_evac, b * 4 + 3)
            if hp == 3 and at.has_batch(-1):
                pe.wait_ge(z_evac, b)
                if at.has_batch(0):
                    pe.wait_ge(v_evac, b * 4 + 4)
                if at.kb % 2 == 1 and not at.first:
                    pe.wait_ge(place_ready, at.trip() + 1)
                for t in range(TC):
                    last = nc.tensor.transpose(M[:, t * P:t * P + P], zT_sb[:, t * P:t * P + P], ident[:])
                last.then_inc(zb_done, 1)
            if hp == 4 and at.has_batch(1):
                v_chunk(at.batch(1), at.bpar(1), 0, r_ready, b)
            if hp == 5 and at.has_batch(-1):
                pe.wait_ge(x1_ready, b)
                j = at.bpar(-1)
                if at.has_batch(1):
                    pe.wait_ge(v_evac, b * 4 + 5)
                for t in range(TC):
                    last = nc.tensor.transpose(M[:, t * P:t * P + P], x1_cur[j][:, t], ident[:])
                last.then_inc(x1T_done, 1)
            if hp == 6 and at.has_batch(-1):
                pe.wait_ge(x1T_evac, b)
                for t in range(TC):
                    last = nc.tensor.matmul(M[:, t * E:t * E + E], x1T_sb[:, t * P:t * P + P], wg_sb[:], start=True, stop=True)
                last.then_inc(logits_done, 1)
            if at.has_route(2):
                t = at.trip()
                pe.wait_ge(onehot_ready, t + 1)
                if at.has_batch(0):
                    pe.wait_ge(v_evac, b * 4 + 4)
                oh = onehot_b[:].rearrange("p t c e -> p (t c) e")
                nc.tensor.matmul(M[:, 0:GROUPS * E], tri[:], oh.rearrange("p g e -> p (g e)"), start=True, stop=False,
                                 skip_group_check=True)
                for g in range(GROUPS):
                    last = nc.tensor.matmul(M[:, (g + 1) * E:(GROUPS + 1) * E].rearrange("p (g e) -> p g e", e=E), ones_b[:],
                                            oh[:, g:g + 1].to_broadcast([P, GROUPS - g, E]), start=False,
                                            stop=(g == GROUPS - 1), skip_group_check=True)
                last.then_inc(prefix_done, 1)
            if hp == 7 and at.has_batch(1):
                if at.has_batch(-1):
                    pe.wait_ge(lg_ready, b)
                v_chunk(at.batch(1), at.bpar(1), 1, v_evac, b * 4 + 5)

        pe.wait_ge(consts, 13)
        pe.wait_ge(w_ready, 4)
        pe.wait_ge(wg_landed, 16)
        project(At(0, 0, True, False), 0)
        v_chunk(0, 0, 0, v_evac, 0)
        v_chunk(0, 0, 1, v_evac, 1)
        trips(pe, step, DRAIN)


def experts_phase(nc, ctx, keep, x1, slot_list, y):
    w1_hi, w3_hi, w2_hi = keep["w_hi"]
    w1_lo, w3_lo, w2_lo = keep["w_lo"]
    count = keep["count"]
    E, F = w1_hi.shape[1:]
    N = x1.shape[0] * x1.shape[1]
    D = x1.shape[2]
    A = F // P
    REGION = N
    RING = 8
    LAG = 6
    TILES = 2 * N // P + E
    TRIPS = TILES // RING
    assert TRIPS * RING == TILES

    def sb(name, shape, dt=F32):
        return ctx.enter_context(nc.sbuf_tensor(name, shape, dt))

    def ps(name):
        return ctx.enter_context(nc.psum_tensor(name, [P, 512], F32))

    def sem(name):
        return ctx.enter_context(nc.semaphore(name))

    ident = sb("ident2", [P, P])
    base_i = sb("base_i", [P, E], I32)
    slot_i = sb("slot_i", [P, TILES, E], I32)
    base_f = sb("base_f", [P, E])
    used = sb("used", [P, E])
    used_i = sb("used_i", [P, E], I32)
    tiles_i = sb("tiles_i", [P, E], I32)
    tiles = sb("tiles", [P, E])
    upto = [sb(f"upto{i}", [P, E]) for i in range(2)]
    jump = sb("jump", [P, E])
    slot_n = sb("slot_n", [P, TILES, E])
    past = sb("past", [P, TILES, E])
    past_j = sb("past_j", [P, TILES, E])
    expert_f = sb("expert_f", [P, TILES])
    row_f = sb("row_f", [P, TILES])
    row_g = sb("row_g", [P, TILES])
    table = sb("table", [P, 2, TILES], I32)
    entry = [sb(f"slots{i}", [P, 3], U32) for i in range(RING)]
    xg = [sb(f"xg{i}", [P, D]) for i in range(RING)]
    xg_hi = [sb(f"xg_hi{i}", [P, P], F32R) for i in range(RING)]
    xg_lo = [sb(f"xg_lo{i}", [P, P], F32R) for i in range(RING)]
    gate = [sb(f"gate{i}", [P, F]) for i in range(2)]
    hid = [sb(f"hid{i}", [P, F]) for i in range(2)]
    hidT_hi = [sb(f"hidT_hi{i}", [P, F], F32R) for i in range(2)]
    hidT_lo = [sb(f"hidT_lo{i}", [P, F], F32R) for i in range(2)]
    y_sb = [sb(f"y_sb{i}", [P, D]) for i in range(RING)]
    H1 = [ps(f"psH1{i}") for i in range(2)]
    H3 = [ps(f"psH3{i}") for i in range(2)]
    XT, HT, YO = ps("psXT"), ps("psHT"), ps("psYO")

    consts = sem("consts2")
    iotas = sem("iotas")
    table_step = sem("table_step")
    table_ready = sem("table_ready")
    slots_landed = [sem(f"slots_landed{i}") for i in range(RING)]
    x_gathered = [sem(f"x_gathered{i}") for i in range(RING)]
    xT_done = sem("xT_done")
    xT_hi_done = sem("xT_hi_done")
    xT_split = sem("xT_split")
    up_done = sem("up_done")
    gate_done = sem("gate_done")
    hid_ready = sem("hid_ready")
    hidT_done = sem("hidT_done")
    hidT_hi_done = sem("hidT_hi_done")
    hidT_split = sem("hidT_split")
    down_done = sem("down_done")
    y_ready = sem("y_ready")
    y_stored = sem("y_stored")

    block = ctx.enter_context(nc.Block())

    def wait(eng, s, value):
        if not isinstance(value, int) or value > 0:
            eng.wait_ge(s, value)

    class At:

        def __init__(self, i, k, first, last):
            self.i, self.k, self.first, self.last = i, k, first, last

        def tile(self, off):
            return self.i * RING + (self.k + off)

        def has(self, off):
            return (not self.first or self.k + off >= 0) and (not self.last or self.k + off < RING)

        def ring(self, off, n=RING):
            return (self.k + off) % n

        def use(self, off):
            return self.i + (self.k + off) // RING

    def trips(eng, step, tail=RING):
        for k in range(RING):
            step(At(0, k, True, False))
        for k in range(RING):
            step(At(1, k, False, False))
        with eng.Fori(2, TRIPS - 1) as i:
            for k in range(RING):
                step(At(i, k, False, False))
        for k in range(RING + tail):
            step(At(TRIPS - 1, k, False, True))

    @block.sync
    def _(sp):
        def load_slots(at, off):
            r = at.ring(off)
            wait(sp, y_stored, (at.tile(off) - RING + 1) * 16)
            row = sp.value_load(table[0:1, 0, bass.ds(at.tile(off), 1)], min_val=0, max_val=E * REGION)
            sp.dma_start(entry[r][:], slot_list[bass.ds(row, P)]).then_inc(slots_landed[r], 16)

        sp.wait_ge(table_ready, 1)
        trips(sp, lambda at: at.has(0) and load_slots(at, 0), 0)

    @block.gpsimd
    def _(pool):
        nc.gpsimd.memset(ident[:], 0.0).then_inc(consts, 1)
        pool.wait_ge(consts, 1)
        nc.gpsimd.affine_select(out=ident[:], in_=ident[:], compare_op=ALU.not_equal, fill=1.0, base=0,
                                pattern=[[-1, P]], channel_multiplier=1).then_inc(consts, 1)
        nc.gpsimd.iota(base_i[:], pattern=[[REGION, E]], base=0, channel_multiplier=0).then_inc(iotas, 1)
        nc.gpsimd.iota(slot_i[:], pattern=[[1, TILES], [0, E]], base=0, channel_multiplier=0).then_inc(iotas, 1)

        def step(at):
            if at.has(0):
                r = at.ring(0)
                wait_alone(pool, consts, (slots_landed[r], at.use(0) * 16 + 16), (xT_done, at.tile(0) - RING + 1))
                nc.gpsimd.indirect_dma_start(out=xg[r][:], out_offset=None, in_=x1.rearrange("b c d -> (b c) d"),
                                             in_offset=bass.IndirectOffsetOnAxis(ap=entry[r][:, 0:1], axis=0)
                                             ).then_inc(x_gathered[r], 16)
            if at.has(-LAG):
                r = at.ring(-LAG)
                wait_alone(pool, consts, (y_ready, at.tile(1 - LAG)), (y_stored, at.tile(-LAG) * 16))
                nc.gpsimd.indirect_dma_start(out=y, out_offset=bass.IndirectOffsetOnAxis(ap=entry[r][:, 1:2], axis=0),
                                             in_=y_sb[r][:], in_offset=None).then_inc(y_stored, 16)

        trips(pool, step)
        pool.wait_ge(y_stored, TILES * 16)

    @block.scalar
    def _(act):
        def x_high(at, off):
            act.wait_ge(xT_done, at.tile(off + 1))
            wait(act, up_done, at.tile(off) - RING + 1)
            nc.scalar.activation(xg_hi[at.ring(off)][:], XT[:, 0:P], ACT.Copy).then_inc(xT_hi_done, 1)

        def step(at):
            if at.has(0):
                j = at.ring(0, 2)
                act.wait_ge(up_done, at.tile(1))
                wait(act, hid_ready, at.tile(-1))
                nc.scalar.activation(gate[j][:], H1[j][:], ACT.Silu).then_inc(gate_done, 1)
            if at.has(2):
                x_high(at, 2)
            if at.has(-2):
                act.wait_ge(down_done, at.tile(-1))
                wait(act, y_stored, (at.tile(-2) - RING + 1) * 16)
                r = at.ring(-2)
                nc.scalar.activation(y_sb[r][:], YO[:, 0:D], ACT.Copy, scale=entry[r][:, 2:3].bitcast(F32)).then_inc(y_ready, 1)
            if at.has(-1):
                j = at.ring(-1, 2)
                act.wait_ge(hidT_done, at.tile(0))
                wait(act, down_done, at.tile(-2))
                nc.scalar.activation(hidT_hi[j][:], HT[:], ACT.Copy).then_inc(hidT_hi_done, 1)

        for n in range(2):
            x_high(At(0, n, True, False), 0)
        trips(act, step)

    @block.vector
    def _(dve):
        n = [0]

        def link(ins):
            n[0] += 1
            ins.then_inc(table_step, 1)
            dve.wait_ge(table_step, n[0])

        dve.wait_ge(iotas, 2)
        link(nc.vector.tensor_copy(base_f[:], base_i[:]))
        link(nc.vector.tensor_tensor(used[:], count[:], base_f[:], ALU.subtract))
        link(nc.vector.tensor_scalar(used_i[:], used[:], float(P - 1), None, ALU.add))
        link(nc.vector.tensor_scalar(tiles_i[:], used_i[:], 7, None, ALU.logical_shift_right))
        link(nc.vector.tensor_copy(tiles[:], tiles_i[:]))
        link(nc.vector.tensor_copy(upto[0][:], tiles[:]))
        for k, d in enumerate((1, 2, 4)):
            a, b = upto[k % 2], upto[(k + 1) % 2]
            nc.vector.tensor_copy(b[:, 0:d], a[:, 0:d])
            link(nc.vector.tensor_tensor(b[:, d:E], a[:, d:E], a[:, 0:E - d], ALU.add))
        total = upto[1]
        link(nc.vector.tensor_scalar(jump[:], tiles[:], -float(P), float(REGION), ALU.mult, ALU.add))
        link(nc.vector.tensor_copy(slot_n[:], slot_i[:]))
        link(nc.vector.tensor_tensor(past[:], slot_n[:], total[:].unsqueeze(1).to_broadcast([P, TILES, E]), ALU.is_ge))
        nc.vector.tensor_reduce(expert_f[:], past[:], AX.X, ALU.add)
        link(nc.vector.tensor_tensor(past_j[:], past[:], jump[:].unsqueeze(1).to_broadcast([P, TILES, E]), ALU.mult))
        link(nc.vector.tensor_reduce(row_f[:], past_j[:], AX.X, ALU.add))
        link(nc.vector.scalar_tensor_tensor(out=row_g[:], in0=slot_n[:, :, 0], scalar=float(P), in1=row_f[:], op0=ALU.mult, op1=ALU.add))
        nc.vector.tensor_scalar(table[:, 0], row_g[:], float(E * REGION), None, ALU.min)
        nc.vector.tensor_scalar(table[:, 1], expert_f[:], float(E - 1), None, ALU.min).then_inc(table_ready, 1)

        def x_low(at, off):
            r = at.ring(off)
            dve.wait_ge(xT_hi_done, at.tile(off + 1))
            nc.vector.tensor_tensor(xg_lo[r][:], XT[:, 0:P], xg_hi[r][:].bitcast(F32), ALU.subtract).then_inc(xT_split, 1)

        def step(at):
            if at.has(0):
                j = at.ring(0, 2)
                dve.wait_ge(gate_done, at.tile(1))
                wait(dve, hidT_done, at.tile(-1))
                nc.vector.tensor_tensor(hid[j][:], H3[j][:], gate[j][:], ALU.mult).then_inc(hid_ready, 1)
            if at.has(2):
                x_low(at, 2)
            if at.has(-1):
                j = at.ring(-1, 2)
                dve.wait_ge(hidT_hi_done, at.tile(0))
                nc.vector.tensor_tensor(hidT_lo[j][:], HT[:], hidT_hi[j][:].bitcast(F32), ALU.subtract).then_inc(hidT_split, 1)

        for k in range(2):
            x_low(At(0, k, True, False), 0)
        trips(dve, step)

    @block.tensor
    def _(pe):
        def transpose_x(at, off):
            r = at.ring(off)
            pe.wait_ge(x_gathered[r], at.use(off) * 16 + 16)
            wait(pe, xT_split, at.tile(off))
            nc.tensor.transpose(XT[:, 0:P], xg[r][:], ident[:]).then_inc(xT_done, 1)

        def expert(at, off):
            return pe.value_load(table[0:1, 1, bass.ds(at.tile(off), 1)], min_val=0, max_val=E - 1)

        def up(at):
            j, r = at.ring(0, 2), at.ring(0)
            e = bass.ds(expert(at, 0), 1)
            pe.wait_ge(xT_split, at.tile(1))
            wait(pe, hid_ready, at.tile(-1))
            for out, hi, lo in ((H1[j], w1_hi, w1_lo), (H3[j], w3_hi, w3_lo)):
                w_h, w_l = (w[:, e].rearrange("p e f -> p (e f)") for w in (hi, lo))
                nc.tensor.matmul(out[:], xg_hi[r][:], w_h, start=True, stop=False)
                nc.tensor.matmul(out[:], xg_lo[r][:], w_h, start=False, stop=False)
                last = nc.tensor.matmul(out[:], xg_hi[r][:], w_l, start=False, stop=True)
            last.then_inc(up_done, 1)

        def transpose_hid(at, off):
            j = at.ring(off, 2)
            pe.wait_ge(hid_ready, at.tile(off + 1))
            wait(pe, hidT_split, at.tile(off))
            for a in range(A):
                last = nc.tensor.transpose(HT[:, a * P:a * P + P], hid[j][:, a * P:a * P + P], ident[:])
            last.then_inc(hidT_done, 1)

        def down(at, off):
            j = at.ring(off, 2)
            e = bass.ds(expert(at, off), 1)
            pe.wait_ge(hidT_split, at.tile(off + 1))
            wait(pe, y_ready, at.tile(off))
            w_h, w_l = (w[:, e].rearrange("p e f -> p (e f)") for w in (w2_hi, w2_lo))
            for a in range(A):
                rows, cols = slice(a * P, a * P + P), slice(a * D, a * D + D)
                nc.tensor.matmul(YO[:, 0:D], hidT_hi[j][:, rows], w_h[:, cols], start=(a == 0), stop=False)
                nc.tensor.matmul(YO[:, 0:D], hidT_lo[j][:, rows], w_h[:, cols], start=False, stop=False)
                last = nc.tensor.matmul(YO[:, 0:D], hidT_hi[j][:, rows], w_l[:, cols], start=False, stop=(a == A - 1))
            last.then_inc(down_done, 1)

        def step(at):
            if at.has(0):
                up(at)
            if at.has(2):
                transpose_x(at, 2)
            if at.has(-2):
                down(at, -2)
            if at.has(-1):
                transpose_hid(at, -1)

        pe.wait_ge(consts, 2)
        pe.wait_ge(table_ready, 1)
        for k in range(2):
            transpose_x(At(0, k, True, False), 0)
        trips(pe, step)


def finish_phase(nc, ctx, x1, y, out):
    NB, C, D = x1.shape
    N = NB * C
    TB = 4
    STEPS = N // (P * TB)

    def sb(name, shape, dt=F32):
        return ctx.enter_context(nc.sbuf_tensor(name, shape, dt))

    def sem(name):
        return ctx.enter_context(nc.semaphore(name))

    R = 4
    xa = [sb(f"xa{i}", [P, TB, D]) for i in range(R)]
    ya = [sb(f"ya{i}", [P, TB, D]) for i in range(R)]
    yb = [sb(f"yb{i}", [P, TB, D]) for i in range(R)]
    s1 = [sb(f"s1{i}", [P, TB, D]) for i in range(2)]
    s2 = [sb(f"s2{i}", [P, TB, D]) for i in range(2)]
    st = [sb(f"st{i}", [P, TB, 6]) for i in range(2)]
    mv = [sb(f"mv2{i}", [P, TB, 2]) for i in range(2)]
    ve = [sb(f"ve{i}", [P, TB]) for i in range(2)]
    rs = [sb(f"rs{i}", [P, TB]) for i in range(2)]
    nm = [sb(f"nm{i}", [P, TB]) for i in range(2)]
    o = [sb(f"o{i}", [P, TB, D]) for i in range(R)]
    neghalf = sb("neghalf2", [P, TB])
    eps = sb("eps2", [P, TB])
    consts = sem("consts3")
    landed = [sem(f"landed{i}") for i in range(R)]
    sum1 = sem("sum1")
    sum2 = sem("sum2")
    st_done = sem("st_done")
    mv_done = sem("mv_done")
    ve_done = sem("ve_done")
    rs_done = sem("rs_done")
    o_ready = sem("o_ready")
    nm_done = sem("nm_done")
    stored = [sem(f"stored{i}") for i in range(R)]
    block = ctx.enter_context(nc.Block())

    def rows(a, n):
        return a[n * P * TB:(n + 1) * P * TB].rearrange("(t p) d -> p t d", p=P)

    xf, of = (a.rearrange("b c d -> (b c) d") for a in (x1, out))

    @block.sync
    def _(sp):
        for n in range(STEPS):
            r = n % R
            if n >= R:
                sp.wait_ge(sum2, n - R + 1)
            sp.dma_start(xa[r][:], rows(xf, n)).then_inc(landed[r], 16)
            sp.dma_start(ya[r][:], rows(y, n)).then_inc(landed[r], 16)
            sp.dma_start(yb[r][:], rows(y[N:2 * N], n)).then_inc(landed[r], 16)

    @block.vector
    def _(dve):
        def shift(n):
            j = n % 2
            dve.wait_ge(rs_done, n + 1)
            nc.vector.scalar_tensor_tensor(out=nm[j][:], in0=mv[j][:, :, 0], scalar=-1.0, in1=rs[j][:], op0=ALU.mult,
                                           op1=ALU.mult).then_inc(nm_done, 1)

        for n in range(STEPS):
            r, j = n % R, n % 2
            dve.wait_ge(landed[r], n // R * 48 + 48)
            nc.vector.tensor_tensor(s1[j][:], xa[r][:], ya[r][:], ALU.add).then_inc(sum1, 1)
            if n:
                shift(n - 1)
            dve.wait_ge(sum1, n + 1)
            if n >= 2:
                dve.wait_ge(o_ready, n - 1)
            nc.vector.tensor_tensor(s2[j][:], s1[j][:], yb[r][:], ALU.add).then_inc(sum2, 1)
            dve.wait_ge(sum2, n + 1)
            for t in range(TB):
                last = nc.vector.bn_stats(st[j][:, t], s2[j][:, t])
            last.then_inc(st_done, 1)
            dve.wait_ge(st_done, n + 1)
            for t in range(TB):
                last = nc.vector.bn_aggr(mv[j][:, t], st[j][:, t])
            last.then_inc(mv_done, 1)
        shift(STEPS - 1)

    @block.gpsimd
    def _(pool):
        nc.gpsimd.memset(neghalf[:], -0.5).then_inc(consts, 1)
        nc.gpsimd.memset(eps[:], EPS).then_inc(consts, 1)
        pool.wait_ge(consts, 2)
        for n in range(STEPS):
            j = n % 2
            pool.wait_ge(mv_done, n + 1)
            nc.gpsimd.tensor_tensor(ve[j][:], mv[j][:, :, 1], eps[:], ALU.add).then_inc(ve_done, 1)
            pool.wait_ge(ve_done, n + 1)
            nc.gpsimd.tensor_tensor(rs[j][:], ve[j][:], neghalf[:], ALU.pow).then_inc(rs_done, 1)

    @block.scalar
    def _(act):
        for n in range(STEPS):
            r, j = n % R, n % 2
            act.wait_ge(nm_done, n + 1)
            if n >= R:
                act.wait_ge(stored[r], n // R * 16)
            for t in range(TB):
                last = nc.scalar.activation(o[r][:, t], s2[j][:, t], ACT.Identity, bias=nm[j][:, t:t + 1], scale=rs[j][:, t:t + 1])
            last.then_inc(o_ready, 1)
            act.wait_ge(o_ready, n + 1)
            act.dma_start(rows(of, n), o[r][:]).then_inc(stored[r], 16)
        for r in range(R):
            act.wait_ge(stored[r], (STEPS - 1 - r) // R * 16 + 16)


def program(nc, xT, x, wq, wk, wv, wz, wg, w1, w3, w2, out):
    NB, C, D = x.shape
    N = NB * C
    E, _, F = w1.shape
    x1 = nc.dram_tensor("x1", [NB, C, D], F32).ap()
    slot_list = nc.dram_tensor("slot_list", [E * N + P, 3], U32).ap()
    y = nc.dram_tensor("y", [2 * N + E * N + P, D], F32).ap()
    with ExitStack() as ctx:
        def sb(name, shape, dt=F32):
            return ctx.enter_context(nc.sbuf_tensor(name, shape, dt))

        keep = {
            "w_hi": [sb(f"f{n}_hi", [P, E, F], F32R) for n in range(3)],
            "w_lo": [sb(f"f{n}_lo", [P, E, F], F32R) for n in range(3)],
            "count": sb("count", [P, E]),
        }
        with ExitStack() as inner:
            attention_phase(nc, inner, keep, xT, x, wq, wk, wv, wz, wg, w1, w3, w2, x1, slot_list)
        with ExitStack() as inner:
            experts_phase(nc, inner, keep, x1, slot_list, y)
        with ExitStack() as inner:
            finish_phase(nc, inner, x1, y, out)


def kernel(**inputs):
    import numpy as _np
    import concourse.bacc as _bacc
    from concourse import mybir as _mybir
    from concourse.bass_utils import run_bass_kernel_spmd as _run

    x = _np.asarray(inputs["L0_attn_x"])
    lay = {
        "xT": x.transpose(0, 2, 1),
        "x": x,
        "wq": _np.asarray(inputs["L0_attn_Q"]).transpose(1, 2, 0).reshape(128, 1024),
        "wk": _np.asarray(inputs["L0_attn_K"]).transpose(1, 2, 0).reshape(128, 1024),
        "wv": _np.asarray(inputs["L0_attn_V"]).transpose(1, 2, 0).reshape(128, 1024),
        "wz": _np.asarray(inputs["L0_attn_W"]).transpose(2, 1, 0).reshape(1024, 128),
        "wg": _np.asarray(inputs["L0_ffn_Wg"]),
        "w1": _np.asarray(inputs["L0_ffn_W1"]),
        "w3": _np.asarray(inputs["L0_ffn_W3"]),
        "w2": _np.asarray(inputs["L0_ffn_W2"]),
    }
    nc = _bacc.Bacc("TRN2", target_bir_lowering=False, num_devices=1)
    arrays, args = {}, []
    for name, a in lay.items():
        a = _np.ascontiguousarray(a)
        arrays[f"in_{name}"] = a
        args.append(nc.dram_tensor(f"in_{name}", a.shape, _mybir.dt.from_np(a.dtype), kind="ExternalInput").ap())
    out = nc.dram_tensor("out_0", x.shape, _mybir.dt.float32, kind="ExternalOutput").ap()
    program(nc, *args, out)
    r = _run(nc, [arrays], core_ids=[0])
    return r.results[0]["out_0"]
```

```python
from contextlib import ExitStack

import concourse.bass as bass
from concourse import mybir

F32 = mybir.dt.float32
F32R = mybir.dt.float32r
BF16 = mybir.dt.bfloat16
I32 = mybir.dt.int32
U32 = mybir.dt.uint32
ALU = mybir.AluOpType
ACT = mybir.ActivationFunctionType
AX = mybir.AxisListType

P = 128
BIG = 1.0e30
EPS = 1e-05


def wait_alone(eng, met, *waits):
    waits = [(s, c if isinstance(c, int) else eng.to_reg(c)) for s, c in waits]
    eng.wait_ge(met, 1)
    for s, c in waits:
        if not isinstance(c, int) or c > 0:
            eng.wait_ge(s, c)


def attention_phase(nc, ctx, keep, xT, x, wq, wk, wv, wz, wg, w1, w3, w2, x1_dram, slot_list):
    NB, C, D = x.shape
    N = NB * C
    E = wg.shape[1]
    F = w1.shape[2]
    GROUPS = 2 * (C // P) * 2
    H, HD = 16, 64
    NP = H // 2
    CHOOSE, ASSIGN, SCATTER = 7, NP + 3, NP + 4
    U_LAG = 2
    UC = 8
    TC = C // P
    TRIPS = NB // 2
    SCALE = 1.0 / P
    RAW = 8
    REGION = N

    def sb(name, shape, dt=F32):
        return ctx.enter_context(nc.sbuf_tensor(name, shape, dt))

    def sem(name):
        return ctx.enter_context(nc.semaphore(name))

    w_raw = sb("w_raw", [P, 4, H * HD])
    wq_hi, wq_lo = sb("wq_hi", [P, H * HD], F32R), sb("wq_lo", [P, H * HD], F32R)
    wk_hi, wk_lo = sb("wk_hi", [P, H * HD], F32R), sb("wk_lo", [P, H * HD], F32R)
    wvz_hi, wvz_lo = sb("wvz_hi", [P, H * D], F32R), sb("wvz_lo", [P, H * D], F32R)
    xT_raw = [sb(f"xT_raw{i}", [P, C]) for i in range(2)]
    xT_hi = [sb(f"xT_hi{i}", [P, C], F32R) for i in range(2)]
    xT_lo = [sb(f"xT_lo{i}", [P, C], F32R) for i in range(2)]
    x_res = [sb(f"x_res{i}", [P, TC, D]) for i in range(2)]
    qk_sb = [sb(f"qk_sb{i}", [P, 2 * C]) for i in range(2)]
    nmax = [sb(f"nmax{i}", [P, 2, 2]) for i in range(2)]
    p_sb = [sb(f"p_sb{i}", [P, 2, 384]) for i in range(2)]
    pT_sb = [sb(f"pT_sb{i}", [P, 2, 384]) for i in range(2)]
    u_sb = [sb(f"u_sb{i}", [P, TC, H * D]) for i in range(2)]
    wv_raw, wz_raw = (u_sb[1][0:HD, t].rearrange("v (h d) -> v h d", d=D) for t in range(2))
    rsum = [sb(f"rsum{i}", [P, 2, 2]) for i in range(2)]
    rinv = [sb(f"rinv{i}", [P, 2, 2]) for i in range(2)]
    r_sb = [sb(f"r_sb{i}", [P, TC, D]) for i in range(2)]
    stats = [sb(f"stats{i}", [P, TC, 6]) for i in range(2)]
    mv = [sb(f"mv{i}", [P, TC, 2]) for i in range(2)]
    veps = [sb(f"veps{i}", [P, TC]) for i in range(2)]
    rstd = [sb(f"rstd{i}", [P, TC]) for i in range(2)]
    x1_cur = [sb(f"x1_cur{i}", [P, TC, D]) for i in range(2)]
    x1T_sb = sb("x1T_sb", [P, C])
    wg_sb = sb("wg_sb", [P, E])
    lg = sb("lg", [P, GROUPS // 2, E])
    top = sb("top", [P, 2, GROUPS // 2])
    eq = sb("eq", [P, GROUPS // 2, E])
    rank = sb("rank", [P, GROUPS // 2])
    lg2 = sb("lg2", [P, GROUPS // 2, E])
    desc = sb("desc", [P, GROUPS // 2, E])
    desc_i = sb("desc_i", [P, GROUPS // 2, E], I32)
    onehot = sb("onehot", [P, GROUPS // 2, 2, E])
    onehot_b = sb("onehot_b", [P, GROUPS // 2, 2, E], BF16)
    gap = sb("gap", [P, GROUPS // 2])
    egap = sb("egap", [P, GROUPS // 2])
    egap1 = sb("egap1", [P, GROUPS // 2])
    place = sb("place", [P, GROUPS, E])
    slot_f = sb("slot_f", [P, GROUPS])
    slot_u = sb("slot_u", [P, GROUPS], U32)
    entry = sb("entry", [P, GROUPS, 3], U32)
    entry_step = sb("entry_step", [P, GROUPS, 2], U32)
    blank = sb("blank", [P, slot_list.shape[0] // P, 3], U32)
    region_i = sb("region_i", [P, E], I32)
    tri = sb("tri", [P, P], BF16)
    ones_b = sb("ones_b", [P, P], BF16)
    x1_cen = [sb(f"x1_cen{i}", [P, TC, D]) for i in range(2)]
    neghalf = sb("neghalf", [P, TC])
    eps = sb("eps", [P, TC])
    ident = sb("ident", [P, P])
    mask = sb("mask", [P, 2 * P])

    S = [ctx.enter_context(nc.psum_tensor(f"psS{i}", [P, 2, 512], F32)) for i in range(2)]
    QK = ctx.enter_context(nc.psum_tensor("psQK", [P, 512], F32))
    Z = [ctx.enter_context(nc.psum_tensor(f"psZ{i}", [P, 512], F32)) for i in range(2)]
    M = ctx.enter_context(nc.psum_tensor("psM", [P, 512], F32))

    WVZ = [S[n // 2][:, n % 2] for n in range(4)]

    w_landed = sem("w_landed")
    wvz_landed = sem("wvz_landed")
    w_hi_done = sem("w_hi_done")
    w_ready = sem("w_ready")
    consts = sem("consts")
    xt_landed = [sem(f"xt_landed{i}") for i in range(2)]
    xr_landed = [sem(f"xr_landed{i}") for i in range(2)]
    xt_hi_done = sem("xt_hi_done")
    xt_split = sem("xt_split")
    qk_done = sem("qk_done")
    qk_evac = sem("qk_evac")
    scores_done = sem("scores_done")
    max_done = sem("max_done")
    p_ready = sem("p_ready")
    pT_done = sem("pT_done")
    pT_evac = sem("pT_evac")
    rinv_done = sem("rinv_done")
    p_scaled = sem("p_scaled")
    z_step = sem("z_step")
    wvz_done = sem("wvz_done")
    wvz_hi_done = sem("wvz_hi_done")
    u_done = sem("u_done")
    u_evac = sem("u_evac")
    r_ready = sem("r_ready")
    bn_done = sem("bn_done")
    stats_done = sem("stats_done")
    veps_done = sem("veps_done")
    rstd_done = sem("rstd_done")
    cen_done = sem("cen_done")
    x1_ready = sem("x1_ready")
    x1T_done = sem("x1T_done")
    x1T_evac = sem("x1T_evac")
    logits_done = sem("logits_done")
    lg_ready = sem("lg_ready")
    wg_landed = sem("wg_landed")
    route_step = sem("route_step")
    onehot_ready = sem("onehot_ready")
    gap_ready = sem("gap_ready")
    egap_ready = sem("egap_ready")
    prefix_done = sem("prefix_done")
    place_ready = sem("place_ready")
    entry_ready = sem("entry_ready")
    scattered = sem("scattered")
    entry_next = sem("entry_next")
    blank_ready = sem("blank_ready")
    blank_stored = sem("blank_stored")
    route_init = sem("route_init")
    f_landed = [sem(f"f_landed{i}") for i in range(RAW)]
    w2_landed = sem("w2_landed")
    f_hi_done = sem("f_hi_done")
    f_ready = sem("f_ready")
    x1_stored = [sem(f"x1_stored{i}") for i in range(2)]

    block = ctx.enter_context(nc.Block())

    def wait(eng, s, count):
        if not isinstance(count, int) or count > 0:
            eng.wait_ge(s, count)

    w_hi, w_lo, count = keep["w_hi"], keep["w_lo"], keep["count"]
    pieces = [(m, e) for m in range(2) for e in range(E)]

    def raw_piece(n):
        n %= RAW
        return w_raw[:, n // 2, (n % 2) * F:(n % 2 + 1) * F]

    class At:

        def __init__(self, i, k, first, last):
            self.i, self.k, self.first, self.last = i, k, first, last
            self.kb, self.hp = k // NP, k % NP

        def pair(self, off):
            return self.i * (2 * NP) + (self.k + off)

        def has(self, off):
            return (not self.first or self.k + off >= 0) and (not self.last or self.k + off < 2 * NP)

        def batch(self, off):
            return self.i * 2 + (self.kb + off)

        def has_batch(self, off):
            return (not self.first or self.kb + off >= 0) and (not self.last or self.kb + off < 2)

        def u_piece(self):
            off = 1 if self.hp >= U_LAG else 0
            if self.has_batch(off) and not (self.first and self.kb + off == 0):
                return off, (self.hp - U_LAG) % UC
            return None

        def has_route(self, hp):
            return self.k % (2 * NP) == hp and not (self.first and self.k < 2 * NP)

        def trip(self):
            return self.i + (self.k // (2 * NP) - 1)

        def hp_of(self, off):
            return (self.k + off) % NP

        def par(self, off):
            return (self.k + off) % 2

        def bpar(self, off):
            return (self.kb + off) % 2

    def trips(eng, step, tail):
        for k in range(2 * NP):
            step(At(0, k, True, False))
        with eng.Fori(1, TRIPS - 1) as i:
            for k in range(2 * NP):
                step(At(i, k, False, False))
        for k in range(2 * NP + tail):
            step(At(TRIPS - 1, k, False, True))

    DRAIN = NP + 5

    @block.sync
    def _(sp):
        def load_xT(b, j):
            sp.dma_start(xT_raw[j][:], xT[bass.ds(b, 1)].rearrange("b p c -> p (b c)")).then_inc(xt_landed[j], 16)

        load_xT(0, 0)
        for n, w in enumerate((wq, wk)):
            sp.dma_start(w_raw[:, n], w).then_inc(w_landed, 16)
        for dst, w in ((wv_raw, wv), (wz_raw, wz)):
            sp.dma_start(dst, w).then_inc(wvz_landed, 16)

        def load_x(b, j):
            sp.dma_start(x_res[j][:], x[bass.ds(b, 1)].rearrange("b (t p) d -> p (b t) d", p=P)).then_inc(xr_landed[j], 16)

        def step(at):
            if at.hp != 0:
                return
            if at.has_batch(2):
                wait(sp, xt_split, at.batch(1))
                load_xT(at.batch(2), at.bpar(2))
            if at.has_batch(-1):
                wait(sp, x1_ready, at.batch(0))
                sp.dma_start(x1_dram[bass.ds(at.batch(-1), 1)].rearrange("b (t p) d -> p (b t) d", p=P),
                             x1_cur[at.bpar(-1)][:]).then_inc(x1_stored[at.bpar(-1)], 16)
            if at.has_batch(1):
                wait(sp, r_ready, at.batch(0))
                load_x(at.batch(1), at.bpar(1))

        load_x(0, 0)
        load_xT(1, 1)
        sp.dma_start(wg_sb[:], wg).then_inc(wg_landed, 16)
        trips(sp, step, 1 + NP)
        for j in range(2):
            sp.wait_ge(x1_stored[j], 16 * TRIPS)

    @block.gpsimd
    def _(pool):
        nc.gpsimd.memset(ident[:], 0.0).then_inc(consts, 1)
        nc.gpsimd.memset(mask[:], 0.0).then_inc(consts, 1)
        nc.gpsimd.memset(tri[:], 1.0).then_inc(consts, 1)
        nc.gpsimd.memset(ones_b[:], 1.0).then_inc(consts, 1)
        nc.gpsimd.memset(neghalf[:], -0.5).then_inc(consts, 1)
        nc.gpsimd.memset(eps[:], EPS).then_inc(consts, 1)
        pool.wait_ge(consts, 6)
        nc.gpsimd.affine_select(out=ident[:], in_=ident[:], compare_op=ALU.not_equal, fill=1.0, base=0,
                                pattern=[[-1, P]], channel_multiplier=1).then_inc(consts, 1)
        nc.gpsimd.affine_select(out=mask[:, P:], in_=mask[:, P:], compare_op=ALU.is_ge, fill=BIG, base=0,
                                pattern=[[-1, P]], channel_multiplier=1).then_inc(consts, 1)

        nc.gpsimd.affine_select(out=tri[:], in_=tri[:], compare_op=ALU.is_gt, fill=0.0, base=0,
                                pattern=[[1, P]], channel_multiplier=-1).then_inc(consts, 1)
        rows = slot_list.shape[0] // P
        nc.gpsimd.memset(blank[:], 0).then_inc(blank_ready, 1)
        pool.wait_ge(blank_ready, 1)
        nc.gpsimd.iota(blank[:, :, 1], pattern=[[1, rows]], base=2 * N, channel_multiplier=rows).then_inc(blank_ready, 1)
        pool.wait_ge(blank_ready, 2)
        pool.dma_start(slot_list.rearrange("(p r) w -> p r w", r=rows), blank[:]).then_inc(blank_stored, 16)
        nc.gpsimd.iota(entry[:, :, 0], pattern=[[P, GROUPS // 2], [0, 2]], base=0, channel_multiplier=1).then_inc(route_init, 1)
        nc.gpsimd.iota(entry[:, :, 1], pattern=[[P, GROUPS // 2], [N, 2]], base=0, channel_multiplier=1).then_inc(route_init, 1)
        nc.gpsimd.iota(entry_step[:], pattern=[[0, GROUPS * 2]], base=P * GROUPS // 2, channel_multiplier=0).then_inc(route_init, 1)
        nc.gpsimd.iota(desc_i[:], pattern=[[0, GROUPS // 2], [-1, E]], base=E, channel_multiplier=0).then_inc(route_init, 1)
        nc.gpsimd.iota(region_i[:], pattern=[[REGION, E]], base=0, channel_multiplier=0).then_inc(route_init, 1)

        def load_piece(n):
            m, e = pieces[n]
            pool.dma_start(raw_piece(n), (w1, w3)[m][e]).then_inc(f_landed[n % RAW], 16)

        def split_piece(n):
            m, e = pieces[n]
            pool.wait_ge(f_hi_done, n + 1)
            nc.gpsimd.tensor_tensor(w_lo[m][:, e], raw_piece(n), w_hi[m][:, e].bitcast(F32), ALU.subtract).then_inc(f_ready, 1)
            if n + RAW < len(pieces):
                pool.wait_ge(f_ready, n + 1)
                load_piece(n + RAW)

        def scatter(t):
            wait_alone(pool, consts, (entry_ready, t + 1))
            for g in range(GROUPS):
                if g:
                    wait_alone(pool, consts, (scattered, (t * GROUPS + g) * 16))
                nc.gpsimd.indirect_dma_start(out=slot_list, out_offset=bass.IndirectOffsetOnAxis(ap=slot_u[:, g:g + 1], axis=0),
                                             in_=entry[:, g], in_offset=None).then_inc(scattered, 16)
            pool.wait_ge(scattered, (t + 1) * (GROUPS * 16))
            nc.gpsimd.tensor_tensor(entry[:, :, 0:2], entry[:, :, 0:2], entry_step[:], ALU.add).then_inc(entry_next, 1)

        def split(b, j, n_trip):
            pool.wait_ge(xt_landed[j], n_trip)
            wait(pool, qk_done, (b - 1) * NP)
            wait(pool, u_done, (b - 1) * UC)
            pool.wait_ge(xt_hi_done, b + 1)
            nc.gpsimd.tensor_tensor(xT_lo[j][:], xT_raw[j][:], xT_hi[j][:].bitcast(F32), ALU.subtract).then_inc(xt_split, 1)

        def step(at):
            if at.first and 2 * at.k < len(pieces):
                for n in (2 * at.k, 2 * at.k + 1):
                    split_piece(n)
            if at.has_route(SCATTER):
                scatter(at.trip())
            if at.hp == NP - 1 and at.has_batch(2):
                split(at.batch(2), at.bpar(2), (at.i + (at.kb + 2) // 2) * 16 + 16)
            if at.hp != 0:
                return
            if at.has_batch(-1):
                j = at.bpar(-1)
                b = at.batch(-1)
                wait(pool, stats_done, b + 1)
                if not (at.first and at.kb < 3):
                    wait(pool, x1_stored[j], at.i * 16 + ((at.kb - 1) // 2) * 16)
                nc.gpsimd.tensor_tensor(veps[j][:], mv[j][:, :, 1], eps[:], ALU.add).then_inc(veps_done, 1)
                pool.wait_ge(veps_done, b + 1)
                nc.gpsimd.tensor_tensor(rstd[j][:], veps[j][:], neghalf[:], ALU.pow).then_inc(rstd_done, 1)
                pool.wait_ge(rstd_done, b + 1)
                nc.gpsimd.tensor_tensor(x1_cen[j][:], r_sb[j][:], mv[j][:, :, 0:1].to_broadcast([P, TC, D]),
                                        ALU.subtract).then_inc(cen_done, 1)
                pool.wait_ge(cen_done, b + 1)
                nc.gpsimd.tensor_tensor(x1_cur[j][:], x1_cen[j][:], rstd[j][:].unsqueeze(2).to_broadcast([P, TC, D]),
                                        ALU.mult).then_inc(x1_ready, 1)

        split(0, 0, 16)
        split(1, 1, 16)
        pool.wait_ge(w_ready, 2)
        for n in range(RAW):
            load_piece(n)
        for e in range(E):
            pool.dma_start(keep["w2"][:, e].rearrange("p (a c) -> p a c", c=D),
                           w2[e].rearrange("(a p) c -> p a c", p=P)).then_inc(w2_landed, 16)
        pool.wait_ge(blank_stored, 16)
        pool.wait_ge(w2_landed, 16 * E)
        trips(pool, step, DRAIN)

    @block.scalar
    def _(act):
        act.wait_ge(w_landed, 32)
        for n, (hi, s) in enumerate(((wq_hi, -SCALE), (wk_hi, 1.0))):
            nc.scalar.activation(hi[:], w_raw[:, n], ACT.Copy, scale=s).then_inc(w_hi_done, 1)

        def qk_copy(at, off):
            n = at.pair(off)
            act.wait_ge(qk_done, n + 1)
            wait(act, scores_done, n - 1)
            nc.scalar.activation(qk_sb[at.par(off)][:], QK[:], ACT.Copy).then_inc(qk_evac, 1)

        def xt_high(b, j, n_trip):
            act.wait_ge(xt_landed[j], n_trip)
            wait(act, qk_done, (b - 1) * NP)
            wait(act, u_done, (b - 1) * UC)
            nc.scalar.activation(xT_hi[j][:], xT_raw[j][:], ACT.Copy).then_inc(xt_hi_done, 1)

        def u_copy(b, j, c):
            act.wait_ge(u_done, b * UC + (c + 1))
            if c == 0:
                wait(act, z_step, (b - 1) * NP)
            t, quarter = c % 2, c // 2
            nc.scalar.activation(u_sb[j][:, t, quarter * 512:quarter * 512 + 512], M[:], ACT.Copy).then_inc(u_evac, 1)

        def step(at):
            if at.has(0):
                n = at.pair(0)
                j = at.par(0)
                wait(act, pT_done, n - 1)
                wait(act, rinv_done, n - 1)
                for h in range(2):
                    act.wait_ge(max_done, n * 4 + (h * 2 + 2))
                    for c, (o, w) in enumerate(((0, 256), (256, 128))):
                        nc.scalar.activation(p_sb[j][:, h, o:o + w], S[j][:, h, o:o + w], ACT.Exp, bias=nmax[j][:, h, c:c + 1],
                                             scale=-1.0, accum_out=rsum[j][:, h, c:c + 1]).then_inc(p_ready, 1)
            if at.has(1):
                qk_copy(at, 1)
            if at.first and 2 * at.k < len(pieces):
                for n in (2 * at.k, 2 * at.k + 1):
                    m, e = pieces[n]
                    act.wait_ge(f_landed[n % RAW], n // RAW * 16 + 16)
                    nc.scalar.activation(w_hi[m][:, e], raw_piece(n), ACT.Copy).then_inc(f_hi_done, 1)
            if at.hp == 4 and at.has_batch(-1):
                act.wait_ge(x1T_done, at.batch(0))
                wait(act, logits_done, at.batch(-1))
                nc.scalar.activation(x1T_sb[:], Z[at.bpar(-1)][:, 0:C], ACT.Copy).then_inc(x1T_evac, 1)
            if at.has_route(CHOOSE):
                act.wait_ge(gap_ready, at.trip() + 1)
                wait(act, entry_ready, at.trip())
                nc.scalar.activation(egap[:], gap[:], ACT.Exp).then_inc(egap_ready, 1)
            if at.hp == NP - 1 and at.has_batch(2):
                xt_high(at.batch(2), at.bpar(2), (at.i + (at.kb + 2) // 2) * 16 + 16)
            if at.u_piece():
                off, c = at.u_piece()
                u_copy(at.batch(off), at.bpar(off), c)

        xt_high(0, 0, 16)
        qk_copy(At(0, 0, True, False), 0)
        xt_high(1, 1, 16)
        act.wait_ge(wvz_done, 1)
        for q in range(4):
            cols = slice(q * 512, q * 512 + 512)
            nc.scalar.activation(wvz_hi[:, cols], WVZ[q], ACT.Copy, scale=1.0 / H).then_inc(wvz_hi_done, 1)
        for c in range(UC):
            u_copy(0, 0, c)
        trips(act, step, DRAIN)

    @block.vector
    def _(dve):
        for n, (hi, lo, s) in enumerate(((wq_hi, wq_lo, -SCALE), (wk_hi, wk_lo, 1.0))):
            dve.wait_ge(w_hi_done, n + 1)
            nc.vector.scalar_tensor_tensor(out=lo[:], in0=w_raw[:, n], scalar=s, in1=hi[:].bitcast(F32),
                                           op0=ALU.mult, op1=ALU.subtract).then_inc(w_ready, 1)

        def step(at):
            if at.has(0):
                n = at.pair(0)
                j = at.par(0)
                wait_alone(dve, consts, (scores_done, n + 1), (p_ready, (n - 1) * 4))
                for h in range(2):
                    for c, (o, w) in enumerate(((0, 256), (256, 128))):
                        s_ap = S[j][:, h, o:o + w]
                        nc.vector.tensor_tensor_reduce(out=s_ap, in0=s_ap, in1=mask[:, 2 * P - w:], scale=1.0, scalar=3.0e38,
                                                       op0=ALU.add, op1=ALU.min, accum_out=nmax[j][:, h, c:c + 1]).then_inc(max_done, 1)
            if at.has(-1):
                n = at.pair(-1)
                j = at.par(-1)
                dve.wait_ge(pT_done, n + 1)
                wait(dve, z_step, n - 1)
                nc.vector.tensor_copy(pT_sb[j][:], S[j][:, :, 0:384]).then_inc(pT_evac, 1)
            if at.has(0):
                n = at.pair(0)
                j = at.par(0)
                dve.wait_ge(p_ready, n * 4 + 4)
                nc.vector.reciprocal(rinv[j][:], rsum[j][:]).then_inc(rinv_done, 1)
                dve.wait_ge(rinv_done, n + 1)
                for h in range(2):
                    for c, (o, w) in enumerate(((0, 256), (256, 128))):
                        p = p_sb[j][:, h, o:o + w]
                        last = nc.vector.tensor_scalar(p, p, rinv[j][:, h, c:c + 1], None, ALU.mult)
                last.then_inc(p_scaled, 1)
            if at.hp == 2 and at.has_batch(-1):
                b, j = at.batch(-1), at.bpar(-1)
                dve.wait_ge(z_step, at.batch(0) * NP)
                dve.wait_ge(xr_landed[j], (at.i + (at.kb - 1) // 2) * 16 + 16)
                wait(dve, x1_ready, b - 1)
                nc.vector.tensor_tensor(r_sb[j][:], Z[j][:, 0:TC * D].rearrange("p (t d) -> p t d", t=TC), x_res[j][:],
                                        ALU.add).then_inc(r_ready, 1)
                dve.wait_ge(r_ready, b + 1)
                for t in range(TC):
                    last = nc.vector.bn_stats(stats[j][:, t], r_sb[j][:, t])
                last.then_inc(bn_done, 1)
                wait_alone(dve, consts, (bn_done, b + 1))
                for t in range(TC):
                    last = nc.vector.bn_aggr(mv[j][:, t], stats[j][:, t])
                last.then_inc(stats_done, 1)

            if at.hp == 5 and at.has_batch(-1):
                jt = at.bpar(-1) * TC
                dve.wait_ge(logits_done, at.batch(0))
                nc.vector.tensor_copy(lg[:, jt:jt + TC], Z[at.bpar(-1)][:, 0:TC * E].rearrange("p (t e) -> p t e", e=E)).then_inc(lg_ready, 1)
            if at.has_route(CHOOSE):
                choose(at.trip())
            if at.has_route(ASSIGN):
                assign(at.trip(), Z[at.bpar(-1)])

        T4 = GROUPS // 2
        STEPS = 16

        def choose(t):
            n = [0]

            def link(ins):
                n[0] += 1
                ins.then_inc(route_step, 1)
                dve.wait_ge(route_step, t * STEPS + n[0])

            def first_of(values, c):
                link(nc.vector.tensor_reduce(top[:, c], values[:], AX.X, ALU.max))
                link(nc.vector.tensor_tensor(eq[:], values[:], top[:, c].unsqueeze(2).to_broadcast([P, T4, E]), ALU.is_equal))
                link(nc.vector.tensor_tensor(lg2[:] if c else eq[:], eq[:], desc[:], ALU.mult))
                link(nc.vector.tensor_reduce(rank[:], (lg2 if c else eq)[:], AX.X, ALU.max))
                link(nc.vector.tensor_tensor(onehot[:, :, c], (lg2 if c else eq)[:],
                                             rank[:].unsqueeze(2).to_broadcast([P, T4, E]), ALU.is_equal))

            dve.wait_ge(lg_ready, t * 2 + 2)
            wait(dve, place_ready, t)
            first_of(lg, 0)
            link(nc.vector.scalar_tensor_tensor(out=lg2[:], in0=onehot[:, :, 0], scalar=-BIG, in1=lg[:], op0=ALU.mult, op1=ALU.add))
            first_of(lg2, 1)
            nc.vector.tensor_copy(onehot_b[:], onehot[:]).then_inc(onehot_ready, 1)
            wait(dve, egap_ready, t)
            nc.vector.tensor_tensor(gap[:], top[:, 1], top[:, 0], ALU.subtract).then_inc(gap_ready, 1)
            assert n[0] == 11

        def assign(t, prefix):
            n = [11]

            def link(ins):
                n[0] += 1
                ins.then_inc(route_step, 1)
                dve.wait_ge(route_step, t * STEPS + n[0])

            counts = prefix[:, 0:(GROUPS + 1) * E].rearrange("p (g e) -> p g e", e=E)
            dve.wait_ge(prefix_done, t + 1)
            wait(dve, entry_next, t)
            link(nc.vector.tensor_tensor(place[:], counts[:, 0:GROUPS], count[:].unsqueeze(1).to_broadcast([P, GROUPS, E]), ALU.add))
            link(nc.vector.tensor_tensor(place[:], place[:], onehot[:].rearrange("p t c e -> p (t c) e"), ALU.mult))
            nc.vector.tensor_tensor(count[:], count[:], counts[:, GROUPS], ALU.add).then_inc(place_ready, 1)
            link(nc.vector.tensor_reduce(slot_f[:], place[:], AX.X, ALU.add))
            nc.vector.tensor_copy(slot_u[:], slot_f[:])
            dve.wait_ge(egap_ready, t + 1)
            link(nc.vector.tensor_scalar(egap1[:], egap[:], 1.0, None, ALU.add))
            w = entry[:].rearrange("p (t c) w -> p t c w", c=2)[:, :, :, 2].bitcast(F32)
            link(nc.vector.reciprocal(w[:, :, 0], egap1[:]))
            nc.vector.tensor_tensor(w[:, :, 1], w[:, :, 0], egap[:], ALU.mult).then_inc(entry_ready, 1)
            assert n[0] == STEPS

        dve.wait_ge(route_init, 5)
        nc.vector.tensor_copy(desc[:], desc_i[:]).then_inc(route_init, 1)
        nc.vector.tensor_copy(count[:], region_i[:]).then_inc(route_init, 1)
        for q in range(4):
            cols = slice(q * 512, q * 512 + 512)
            dve.wait_ge(wvz_hi_done, q + 1)
            nc.vector.scalar_tensor_tensor(out=wvz_lo[:, cols], in0=WVZ[q], scalar=1.0 / H, in1=wvz_hi[:, cols].bitcast(F32),
                                           op0=ALU.mult, op1=ALU.subtract).then_inc(w_ready, 1)
        dve.wait_ge(route_init, 7)
        trips(dve, step, DRAIN)

    @block.tensor
    def _(pe):
        def project(at, off):
            n = at.pair(off)
            cols = slice(at.hp_of(off) * P, at.hp_of(off) * P + P)
            b_off = (at.k + off) // NP - at.kb
            if at.hp_of(off) == 0:
                pe.wait_ge(xt_split, at.batch(b_off) + 1)
            wait(pe, qk_evac, n)
            j = at.bpar(b_off)
            for o, hi, lo in ((0, wq_hi, wq_lo), (C, wk_hi, wk_lo)):
                out = QK[:, o:o + C]
                nc.tensor.matmul(out, hi[:, cols], xT_hi[j][:], start=True, stop=False)
                nc.tensor.matmul(out, lo[:, cols], xT_hi[j][:], start=False, stop=False)
                last = nc.tensor.matmul(out, hi[:, cols], xT_lo[j][:], start=False, stop=True)
            last.then_inc(qk_done, 1)

        def scores(at):
            n = at.pair(0)
            j = at.par(0)
            wait(pe, pT_evac, n - 1)
            pe.wait_ge(qk_evac, n + 1)
            for o, q0, nk in ((0, P, 2 * P), (2 * P, 0, P)):
                for h in range(2):
                    r = slice(h * HD, h * HD + HD)
                    last = nc.tensor.matmul(S[j][:, h, o:o + nk], qk_sb[j][r, q0:q0 + P], qk_sb[j][r, C:C + nk], start=True, stop=True)
            last.then_inc(scores_done, 1)

        def transpose_p(at, off):
            n = at.pair(off)
            j = at.par(off)
            pe.wait_ge(p_scaled, n + 1)
            for h in range(2):
                for c in range(3):
                    last = nc.tensor.transpose(S[j][:, h, c * P:c * P + P], p_sb[j][:, h, c * P:c * P + P], ident[:])
            last.then_inc(pT_done, 1)

        def values(at, off):
            n = at.pair(off)
            j = at.par(off)
            hp = at.hp_of(off)
            b_off = (at.k + off) // NP - at.kb
            b = at.batch(b_off)
            jb = at.bpar(b_off)
            wait_u = hp % 2 == 0
            if wait_u:
                pe.wait_ge(u_evac, b * UC + (hp + 2))
            if hp == 0:
                wait(pe, r_ready, b - 1)
            pe.wait_ge(pT_evac, n + 1)
            for h in range(2):
                cols = slice((2 * hp + h) * D, (2 * hp + h + 1) * D)
                for t, block, tu in ((0, 2, 0), (1, 0, 0), (1, 1, 1)):
                    last = nc.tensor.matmul(Z[jb][:, t * D:t * D + D], pT_sb[j][:, h, block * P:block * P + P],
                                            u_sb[jb][:, tu, cols], start=(hp == 0 and h == 0 and t == 0),
                                            stop=(hp == NP - 1 and h == 1), skip_group_check=True)
            last.then_inc(z_step, 1)

        def u_chunk(b, j, c):
            wait(pe, u_evac, b * UC + c)
            pe.wait_ge(xt_split, b + 1)
            t, quarter = c % 2, c // 2
            cols = slice(quarter * 512, quarter * 512 + 512)
            rows = slice(t * P, t * P + P)
            nc.tensor.matmul(M[:], xT_hi[j][:, rows], wvz_hi[:, cols], start=True, stop=False)
            nc.tensor.matmul(M[:], xT_lo[j][:, rows], wvz_hi[:, cols], start=False, stop=False)
            nc.tensor.matmul(M[:], xT_hi[j][:, rows], wvz_lo[:, cols], start=False, stop=True).then_inc(u_done, 1)

        def step(at):
            if at.has(0):
                scores(at)
            if at.has(1):
                project(at, 1)
            b, hp = at.batch(0), at.hp

            aux = Z[at.bpar(-1)]
            if hp == 4 and at.has_batch(-1):
                pe.wait_ge(x1_ready, b)
                if at.kb % 2 == 1 and not at.first:
                    pe.wait_ge(place_ready, at.trip() + 1)
                j = at.bpar(-1)
                for t in range(TC):
                    last = nc.tensor.transpose(aux[:, t * P:t * P + P], x1_cur[j][:, t], ident[:])
                last.then_inc(x1T_done, 1)
            if hp == 5 and at.has_batch(-1):
                pe.wait_ge(x1T_evac, b)
                for t in range(TC):
                    last = nc.tensor.matmul(aux[:, t * E:t * E + E], x1T_sb[:, t * P:t * P + P], wg_sb[:], start=True, stop=True)
                last.then_inc(logits_done, 1)
            if at.has_route(ASSIGN):
                pe.wait_ge(onehot_ready, at.trip() + 1)
                if at.has_batch(-1):
                    pe.wait_ge(r_ready, b)
                oh = onehot_b[:].rearrange("p t c e -> p (t c) e")
                nc.tensor.matmul(aux[:, 0:GROUPS * E], tri[:], oh.rearrange("p g e -> p (g e)"), start=True, stop=False,
                                 skip_group_check=True)
                for g in range(GROUPS):
                    last = nc.tensor.matmul(aux[:, (g + 1) * E:(GROUPS + 1) * E].rearrange("p (g e) -> p g e", e=E), ones_b[:],
                                            oh[:, g:g + 1].to_broadcast([P, GROUPS - g, E]), start=False,
                                            stop=(g == GROUPS - 1), skip_group_check=True)
                last.then_inc(prefix_done, 1)
            if at.has(-1):
                transpose_p(at, -1)
            if at.has(-2):
                values(at, -2)
            if at.u_piece():
                off, c = at.u_piece()
                u_chunk(at.batch(off), at.bpar(off), c)

        pe.wait_ge(consts, 9)
        pe.wait_ge(wvz_landed, 32)
        for h in range(H):
            last = nc.tensor.matmul(WVZ[h // 4][:, h % 4 * D:h % 4 * D + D], wv_raw[:, h], wz_raw[:, h], start=True, stop=True)
        last.then_inc(wvz_done, 1)
        pe.wait_ge(w_ready, 2)
        pe.wait_ge(wg_landed, 16)
        project(At(0, 0, True, False), 0)
        pe.wait_ge(w_ready, 6)
        for c in range(UC):
            u_chunk(0, 0, c)
        trips(pe, step, DRAIN)


def experts_phase(nc, ctx, keep, x1, slot_list, y):
    w1_hi, w3_hi = keep["w_hi"]
    w1_lo, w3_lo = keep["w_lo"]
    w2 = keep["w2"]
    count = keep["count"]
    E, F = w1_hi.shape[1:]
    N = x1.shape[0] * x1.shape[1]
    D = x1.shape[2]
    A = F // P
    REGION = N
    RING = 8
    LAG = 6
    TILES = 2 * N // P + E
    TRIPS = TILES // RING
    assert TRIPS * RING == TILES

    def sb(name, shape, dt=F32):
        return ctx.enter_context(nc.sbuf_tensor(name, shape, dt))

    def ps(name):
        return ctx.enter_context(nc.psum_tensor(name, [P, 512], F32))

    def sem(name):
        return ctx.enter_context(nc.semaphore(name))

    ident = sb("ident2", [P, P])
    base_i = sb("base_i", [P, E], I32)
    slot_i = sb("slot_i", [P, TILES, E], I32)
    base_f = sb("base_f", [P, E])
    used = sb("used", [P, E])
    used_i = sb("used_i", [P, E], I32)
    tiles_i = sb("tiles_i", [P, E], I32)
    tiles = sb("tiles", [P, E])
    upto = [sb(f"upto{i}", [P, E]) for i in range(2)]
    jump = sb("jump", [P, E])
    slot_n = sb("slot_n", [P, TILES, E])
    past = sb("past", [P, TILES, E])
    past_j = sb("past_j", [P, TILES, E])
    expert_f = sb("expert_f", [P, TILES])
    row_f = sb("row_f", [P, TILES])
    row_g = sb("row_g", [P, TILES])
    table = sb("table", [P, 2, TILES], I32)
    entry = [sb(f"slots{i}", [P, 3], U32) for i in range(RING)]
    xg = [sb(f"xg{i}", [P, D]) for i in range(RING)]
    xg_hi = [sb(f"xg_hi{i}", [P, P], F32R) for i in range(RING)]
    xg_lo = [sb(f"xg_lo{i}", [P, P], F32R) for i in range(RING)]
    gate = [sb(f"gate{i}", [P, F]) for i in range(2)]
    hid = [sb(f"hid{i}", [P, F]) for i in range(2)]
    hidT_sb = [sb(f"hidT_sb{i}", [P, F]) for i in range(2)]
    y_sb = [sb(f"y_sb{i}", [P, D]) for i in range(RING)]
    H1 = [ps(f"psH1{i}") for i in range(2)]
    H3 = [ps(f"psH3{i}") for i in range(2)]
    XT, HT, YO = ps("psXT"), ps("psHT"), ps("psYO")

    consts = sem("consts2")
    iotas = sem("iotas")
    table_step = sem("table_step")
    table_ready = sem("table_ready")
    slots_landed = [sem(f"slots_landed{i}") for i in range(RING)]
    x_gathered = [sem(f"x_gathered{i}") for i in range(RING)]
    xT_done = sem("xT_done")
    xT_hi_done = sem("xT_hi_done")
    xT_split = sem("xT_split")
    up_done = sem("up_done")
    gate_done = sem("gate_done")
    hid_ready = sem("hid_ready")
    hidT_done = sem("hidT_done")
    hidT_evac = sem("hidT_evac")
    down_done = sem("down_done")
    y_ready = sem("y_ready")
    y_stored = sem("y_stored")

    block = ctx.enter_context(nc.Block())

    def wait(eng, s, value):
        if not isinstance(value, int) or value > 0:
            eng.wait_ge(s, value)

    class At:

        def __init__(self, i, k, first, last):
            self.i, self.k, self.first, self.last = i, k, first, last

        def tile(self, off):
            return self.i * RING + (self.k + off)

        def has(self, off):
            return (not self.first or self.k + off >= 0) and (not self.last or self.k + off < RING)

        def ring(self, off, n=RING):
            return (self.k + off) % n

        def use(self, off):
            return self.i + (self.k + off) // RING

    def trips(eng, step, tail=RING):
        for k in range(RING):
            step(At(0, k, True, False))
        for k in range(RING):
            step(At(1, k, False, False))
        with eng.Fori(2, TRIPS - 1) as i:
            for k in range(RING):
                step(At(i, k, False, False))
        for k in range(RING + tail):
            step(At(TRIPS - 1, k, False, True))

    @block.sync
    def _(sp):
        def load_slots(at, off):
            r = at.ring(off)
            wait(sp, y_stored, (at.tile(off) - RING + 1) * 16)
            row = sp.value_load(table[0:1, 0, bass.ds(at.tile(off), 1)], min_val=0, max_val=E * REGION)
            sp.dma_start(entry[r][:], slot_list[bass.ds(row, P)]).then_inc(slots_landed[r], 16)

        sp.wait_ge(table_ready, 1)
        trips(sp, lambda at: at.has(0) and load_slots(at, 0), 0)

    @block.gpsimd
    def _(pool):
        nc.gpsimd.memset(ident[:], 0.0).then_inc(consts, 1)
        pool.wait_ge(consts, 1)
        nc.gpsimd.affine_select(out=ident[:], in_=ident[:], compare_op=ALU.not_equal, fill=1.0, base=0,
                                pattern=[[-1, P]], channel_multiplier=1).then_inc(consts, 1)
        nc.gpsimd.iota(base_i[:], pattern=[[REGION, E]], base=0, channel_multiplier=0).then_inc(iotas, 1)
        nc.gpsimd.iota(slot_i[:], pattern=[[1, TILES], [0, E]], base=0, channel_multiplier=0).then_inc(iotas, 1)

        def step(at):
            if at.has(0):
                r = at.ring(0)
                wait_alone(pool, consts, (slots_landed[r], at.use(0) * 16 + 16), (xT_done, at.tile(0) - RING + 1))
                nc.gpsimd.indirect_dma_start(out=xg[r][:], out_offset=None, in_=x1.rearrange("b c d -> (b c) d"),
                                             in_offset=bass.IndirectOffsetOnAxis(ap=entry[r][:, 0:1], axis=0)
                                             ).then_inc(x_gathered[r], 16)
            if at.has(-LAG):
                r = at.ring(-LAG)
                wait_alone(pool, consts, (y_ready, at.tile(1 - LAG)), (y_stored, at.tile(-LAG) * 16))
                nc.gpsimd.indirect_dma_start(out=y, out_offset=bass.IndirectOffsetOnAxis(ap=entry[r][:, 1:2], axis=0),
                                             in_=y_sb[r][:], in_offset=None).then_inc(y_stored, 16)

        trips(pool, step)
        pool.wait_ge(y_stored, TILES * 16)

    @block.scalar
    def _(act):
        def x_high(at, off):
            act.wait_ge(xT_done, at.tile(off + 1))
            wait(act, up_done, at.tile(off) - RING + 1)
            nc.scalar.activation(xg_hi[at.ring(off)][:], XT[:, 0:P], ACT.Copy).then_inc(xT_hi_done, 1)

        def step(at):
            if at.has(0):
                j = at.ring(0, 2)
                act.wait_ge(up_done, at.tile(1))
                wait(act, hid_ready, at.tile(-1))
                nc.scalar.activation(gate[j][:], H1[j][:], ACT.Silu).then_inc(gate_done, 1)
            if at.has(2):
                x_high(at, 2)
            if at.has(-2):
                act.wait_ge(down_done, at.tile(-1))
                wait(act, y_stored, (at.tile(-2) - RING + 1) * 16)
                r = at.ring(-2)
                nc.scalar.activation(y_sb[r][:], YO[:, 0:D], ACT.Copy, scale=entry[r][:, 2:3].bitcast(F32)).then_inc(y_ready, 1)
            if at.has(-1):
                j = at.ring(-1, 2)
                act.wait_ge(hidT_done, at.tile(0))
                wait(act, down_done, at.tile(-2))
                nc.scalar.activation(hidT_sb[j][:], HT[:], ACT.Copy).then_inc(hidT_evac, 1)

        for n in range(2):
            x_high(At(0, n, True, False), 0)
        trips(act, step)

    @block.vector
    def _(dve):
        n = [0]

        def link(ins):
            n[0] += 1
            ins.then_inc(table_step, 1)
            dve.wait_ge(table_step, n[0])

        dve.wait_ge(iotas, 2)
        link(nc.vector.tensor_copy(base_f[:], base_i[:]))
        link(nc.vector.tensor_tensor(used[:], count[:], base_f[:], ALU.subtract))
        link(nc.vector.tensor_scalar(used_i[:], used[:], float(P - 1), None, ALU.add))
        link(nc.vector.tensor_scalar(tiles_i[:], used_i[:], 7, None, ALU.logical_shift_right))
        link(nc.vector.tensor_copy(tiles[:], tiles_i[:]))
        link(nc.vector.tensor_copy(upto[0][:], tiles[:]))
        for k, d in enumerate((1, 2, 4)):
            a, b = upto[k % 2], upto[(k + 1) % 2]
            nc.vector.tensor_copy(b[:, 0:d], a[:, 0:d])
            link(nc.vector.tensor_tensor(b[:, d:E], a[:, d:E], a[:, 0:E - d], ALU.add))
        total = upto[1]
        link(nc.vector.tensor_scalar(jump[:], tiles[:], -float(P), float(REGION), ALU.mult, ALU.add))
        link(nc.vector.tensor_copy(slot_n[:], slot_i[:]))
        link(nc.vector.tensor_tensor(past[:], slot_n[:], total[:].unsqueeze(1).to_broadcast([P, TILES, E]), ALU.is_ge))
        nc.vector.tensor_reduce(expert_f[:], past[:], AX.X, ALU.add)
        link(nc.vector.tensor_tensor(past_j[:], past[:], jump[:].unsqueeze(1).to_broadcast([P, TILES, E]), ALU.mult))
        link(nc.vector.tensor_reduce(row_f[:], past_j[:], AX.X, ALU.add))
        link(nc.vector.scalar_tensor_tensor(out=row_g[:], in0=slot_n[:, :, 0], scalar=float(P), in1=row_f[:], op0=ALU.mult, op1=ALU.add))
        nc.vector.tensor_scalar(table[:, 0], row_g[:], float(E * REGION), None, ALU.min)
        nc.vector.tensor_scalar(table[:, 1], expert_f[:], float(E - 1), None, ALU.min).then_inc(table_ready, 1)

        def x_low(at, off):
            r = at.ring(off)
            dve.wait_ge(xT_hi_done, at.tile(off + 1))
            nc.vector.tensor_tensor(xg_lo[r][:], XT[:, 0:P], xg_hi[r][:].bitcast(F32), ALU.subtract).then_inc(xT_split, 1)

        def step(at):
            if at.has(0):
                j = at.ring(0, 2)
                dve.wait_ge(gate_done, at.tile(1))
                wait(dve, hidT_done, at.tile(-1))
                nc.vector.tensor_tensor(hid[j][:], H3[j][:], gate[j][:], ALU.mult).then_inc(hid_ready, 1)
            if at.has(2):
                x_low(at, 2)

        for k in range(2):
            x_low(At(0, k, True, False), 0)
        trips(dve, step)

    @block.tensor
    def _(pe):
        def transpose_x(at, off):
            r = at.ring(off)
            pe.wait_ge(x_gathered[r], at.use(off) * 16 + 16)
            wait(pe, xT_split, at.tile(off))
            nc.tensor.transpose(XT[:, 0:P], xg[r][:], ident[:]).then_inc(xT_done, 1)

        def expert(at, off):
            return pe.value_load(table[0:1, 1, bass.ds(at.tile(off), 1)], min_val=0, max_val=E - 1)

        def up(at):
            j, r = at.ring(0, 2), at.ring(0)
            e = bass.ds(expert(at, 0), 1)
            pe.wait_ge(xT_split, at.tile(1))
            wait(pe, hid_ready, at.tile(-1))
            for out, hi, lo in ((H1[j], w1_hi, w1_lo), (H3[j], w3_hi, w3_lo)):
                w_h, w_l = (w[:, e].rearrange("p e f -> p (e f)") for w in (hi, lo))
                nc.tensor.matmul(out[:], xg_hi[r][:], w_h, start=True, stop=False)
                nc.tensor.matmul(out[:], xg_lo[r][:], w_h, start=False, stop=False)
                last = nc.tensor.matmul(out[:], xg_hi[r][:], w_l, start=False, stop=True)
            last.then_inc(up_done, 1)

        def transpose_hid(at, off):
            j = at.ring(off, 2)
            pe.wait_ge(hid_ready, at.tile(off + 1))
            wait(pe, hidT_evac, at.tile(off))
            for a in range(A):
                last = nc.tensor.transpose(HT[:, a * P:a * P + P], hid[j][:, a * P:a * P + P], ident[:])
            last.then_inc(hidT_done, 1)

        def down(at, off):
            j = at.ring(off, 2)
            e = bass.ds(expert(at, off), 1)
            pe.wait_ge(hidT_evac, at.tile(off + 1))
            wait(pe, y_ready, at.tile(off))
            w = w2[:, e].rearrange("p e f -> p (e f)")
            for a in range(A):
                last = nc.tensor.matmul(YO[:, 0:D], hidT_sb[j][:, a * P:a * P + P], w[:, a * D:a * D + D],
                                        start=(a == 0), stop=(a == A - 1))
            last.then_inc(down_done, 1)

        def step(at):
            if at.has(0):
                up(at)
            if at.has(2):
                transpose_x(at, 2)
            if at.has(-2):
                down(at, -2)
            if at.has(-1):
                transpose_hid(at, -1)

        pe.wait_ge(consts, 2)
        pe.wait_ge(table_ready, 1)
        for k in range(2):
            transpose_x(At(0, k, True, False), 0)
        trips(pe, step)


def finish_phase(nc, ctx, x1, y, out):
    NB, C, D = x1.shape
    N = NB * C
    TB = 4
    STEPS = N // (P * TB)

    def sb(name, shape, dt=F32):
        return ctx.enter_context(nc.sbuf_tensor(name, shape, dt))

    def sem(name):
        return ctx.enter_context(nc.semaphore(name))

    R = 4
    xa = [sb(f"xa{i}", [P, TB, D]) for i in range(R)]
    ya = [sb(f"ya{i}", [P, TB, D]) for i in range(R)]
    yb = [sb(f"yb{i}", [P, TB, D]) for i in range(R)]
    s1 = [sb(f"s1{i}", [P, TB, D]) for i in range(2)]
    s2 = [sb(f"s2{i}", [P, TB, D]) for i in range(2)]
    st = [sb(f"st{i}", [P, TB, 6]) for i in range(2)]
    mv = [sb(f"mv2{i}", [P, TB, 2]) for i in range(2)]
    ve = [sb(f"ve{i}", [P, TB]) for i in range(2)]
    rs = [sb(f"rs{i}", [P, TB]) for i in range(2)]
    nm = [sb(f"nm{i}", [P, TB]) for i in range(2)]
    o = [sb(f"o{i}", [P, TB, D]) for i in range(R)]
    neghalf = sb("neghalf2", [P, TB])
    eps = sb("eps2", [P, TB])
    consts = sem("consts3")
    landed = [sem(f"landed{i}") for i in range(R)]
    sum1 = sem("sum1")
    sum2 = sem("sum2")
    st_done = sem("st_done")
    mv_done = sem("mv_done")
    ve_done = sem("ve_done")
    rs_done = sem("rs_done")
    o_ready = sem("o_ready")
    nm_done = sem("nm_done")
    stored = [sem(f"stored{i}") for i in range(R)]
    block = ctx.enter_context(nc.Block())

    def rows(a, n):
        return a[n * P * TB:(n + 1) * P * TB].rearrange("(t p) d -> p t d", p=P)

    xf, of = (a.rearrange("b c d -> (b c) d") for a in (x1, out))

    @block.sync
    def _(sp):
        for n in range(STEPS):
            r = n % R
            if n >= R:
                sp.wait_ge(sum2, n - R + 1)
            sp.dma_start(xa[r][:], rows(xf, n)).then_inc(landed[r], 16)
            sp.dma_start(ya[r][:], rows(y, n)).then_inc(landed[r], 16)
            sp.dma_start(yb[r][:], rows(y[N:2 * N], n)).then_inc(landed[r], 16)

    @block.vector
    def _(dve):
        def shift(n):
            j = n % 2
            dve.wait_ge(rs_done, n + 1)
            nc.vector.scalar_tensor_tensor(out=nm[j][:], in0=mv[j][:, :, 0], scalar=-1.0, in1=rs[j][:], op0=ALU.mult,
                                           op1=ALU.mult).then_inc(nm_done, 1)

        for n in range(STEPS):
            r, j = n % R, n % 2
            dve.wait_ge(landed[r], n // R * 48 + 48)
            nc.vector.tensor_tensor(s1[j][:], xa[r][:], ya[r][:], ALU.add).then_inc(sum1, 1)
            if n:
                shift(n - 1)
            dve.wait_ge(sum1, n + 1)
            if n >= 2:
                dve.wait_ge(o_ready, n - 1)
            nc.vector.tensor_tensor(s2[j][:], s1[j][:], yb[r][:], ALU.add).then_inc(sum2, 1)
            dve.wait_ge(sum2, n + 1)
            for t in range(TB):
                last = nc.vector.bn_stats(st[j][:, t], s2[j][:, t])
            last.then_inc(st_done, 1)
            dve.wait_ge(st_done, n + 1)
            for t in range(TB):
                last = nc.vector.bn_aggr(mv[j][:, t], st[j][:, t])
            last.then_inc(mv_done, 1)
        shift(STEPS - 1)

    @block.gpsimd
    def _(pool):
        nc.gpsimd.memset(neghalf[:], -0.5).then_inc(consts, 1)
        nc.gpsimd.memset(eps[:], EPS).then_inc(consts, 1)
        pool.wait_ge(consts, 2)
        for n in range(STEPS):
            j = n % 2
            pool.wait_ge(mv_done, n + 1)
            nc.gpsimd.tensor_tensor(ve[j][:], mv[j][:, :, 1], eps[:], ALU.add).then_inc(ve_done, 1)
            pool.wait_ge(ve_done, n + 1)
            nc.gpsimd.tensor_tensor(rs[j][:], ve[j][:], neghalf[:], ALU.pow).then_inc(rs_done, 1)

    @block.scalar
    def _(act):
        for n in range(STEPS):
            r, j = n % R, n % 2
            act.wait_ge(nm_done, n + 1)
            if n >= R:
                act.wait_ge(stored[r], n // R * 16)
            for t in range(TB):
                last = nc.scalar.activation(o[r][:, t], s2[j][:, t], ACT.Identity, bias=nm[j][:, t:t + 1], scale=rs[j][:, t:t + 1])
            last.then_inc(o_ready, 1)
            act.wait_ge(o_ready, n + 1)
            act.dma_start(rows(of, n), o[r][:]).then_inc(stored[r], 16)
        for r in range(R):
            act.wait_ge(stored[r], (STEPS - 1 - r) // R * 16 + 16)


def program(nc, xT, x, wq, wk, wv, wz, wg, w1, w3, w2, out):
    NB, C, D = x.shape
    N = NB * C
    E, _, F = w1.shape
    x1 = nc.dram_tensor("x1", [NB, C, D], F32).ap()
    slot_list = nc.dram_tensor("slot_list", [E * N + P, 3], U32).ap()
    y = nc.dram_tensor("y", [2 * N + E * N + P, D], F32).ap()
    with ExitStack() as ctx:
        def sb(name, shape, dt=F32):
            return ctx.enter_context(nc.sbuf_tensor(name, shape, dt))

        keep = {
            "w_hi": [sb(f"f{n}_hi", [P, E, F], F32R) for n in range(2)],
            "w_lo": [sb(f"f{n}_lo", [P, E, F], F32R) for n in range(2)],
            "w2": sb("f2", [P, E, F]),
            "count": sb("count", [P, E]),
        }
        with ExitStack() as inner:
            attention_phase(nc, inner, keep, xT, x, wq, wk, wv, wz, wg, w1, w3, w2, x1, slot_list)
        with ExitStack() as inner:
            experts_phase(nc, inner, keep, x1, slot_list, y)
        with ExitStack() as inner:
            finish_phase(nc, inner, x1, y, out)


def kernel(**inputs):
    import numpy as _np
    import concourse.bacc as _bacc
    from concourse import mybir as _mybir
    from concourse.bass_utils import run_bass_kernel_spmd as _run

    x = _np.asarray(inputs["L0_attn_x"])
    lay = {
        "xT": x.transpose(0, 2, 1),
        "x": x,
        "wq": _np.asarray(inputs["L0_attn_Q"]).transpose(1, 2, 0).reshape(128, 1024),
        "wk": _np.asarray(inputs["L0_attn_K"]).transpose(1, 2, 0).reshape(128, 1024),
        "wv": _np.asarray(inputs["L0_attn_V"]).transpose(0, 2, 1),
        "wz": _np.asarray(inputs["L0_attn_W"]).transpose(1, 2, 0),
        "wg": _np.asarray(inputs["L0_ffn_Wg"]),
        "w1": _np.asarray(inputs["L0_ffn_W1"]),
        "w3": _np.asarray(inputs["L0_ffn_W3"]),
        "w2": _np.asarray(inputs["L0_ffn_W2"]),
    }
    nc = _bacc.Bacc("TRN2", target_bir_lowering=False, num_devices=1)
    arrays, args = {}, []
    for name, a in lay.items():
        a = _np.ascontiguousarray(a)
        arrays[f"in_{name}"] = a
        args.append(nc.dram_tensor(f"in_{name}", a.shape, _mybir.dt.from_np(a.dtype), kind="ExternalInput").ap())
    out = nc.dram_tensor("out_0", x.shape, _mybir.dt.float32, kind="ExternalOutput").ap()
    program(nc, *args, out)
    r = _run(nc, [arrays], core_ids=[0])
    return r.results[0]["out_0"]
```

```python
from contextlib import ExitStack

import concourse.bass as bass
from concourse import mybir

F32 = mybir.dt.float32
F32R = mybir.dt.float32r
BF16 = mybir.dt.bfloat16
I32 = mybir.dt.int32
U32 = mybir.dt.uint32
ALU = mybir.AluOpType
ACT = mybir.ActivationFunctionType
AX = mybir.AxisListType

P = 128
BIG = 1.0e30
EPS = 1e-05


def wait_alone(eng, met, *waits):
    waits = [(s, c if isinstance(c, int) else eng.to_reg(c)) for s, c in waits]
    eng.wait_ge(met, 1)
    for s, c in waits:
        if not isinstance(c, int) or c > 0:
            eng.wait_ge(s, c)


def attention_phase(nc, ctx, keep, xT, x, wq, wk, wv, wz, wg, w1, w3, w2, x1_dram, slot_list):
    NB, C, D = x.shape
    N = NB * C
    E = wg.shape[1]
    F = w1.shape[2]
    GROUPS = 2 * (C // P) * 2
    HD = wv.shape[0]
    H = wv.shape[1]
    NP = H // 2
    CHOOSE, ASSIGN, SCATTER = NP - 2, NP, NP
    U_LAG = 2
    UC = 8
    TC = C // P
    TRIPS = NB // 2
    SCALE = 1.0 / P
    RAW = 8
    REGION = N

    def sb(name, shape, dt=F32):
        return ctx.enter_context(nc.sbuf_tensor(name, shape, dt))

    def sem(name):
        return ctx.enter_context(nc.semaphore(name))

    w_raw = sb("w_raw", [P, 4, H * HD])
    wqk_hi, wqk_lo = sb("wqk_hi", [P, H * D], F32R), sb("wqk_lo", [P, H * D], F32R)
    wvz_hi, wvz_lo = sb("wvz_hi", [P, H * D], F32R), sb("wvz_lo", [P, H * D], F32R)
    xT_raw = [sb(f"xT_raw{i}", [P, C]) for i in range(2)]
    xT_hi = [sb(f"xT_hi{i}", [P, C], F32R) for i in range(2)]
    xT_lo = [sb(f"xT_lo{i}", [P, C], F32R) for i in range(2)]
    x_res = [sb(f"x_res{i}", [P, TC, D]) for i in range(2)]
    t_hi = [sb(f"t_hi{i}", [P, 2 * C], F32R) for i in range(2)]
    t_lo = [sb(f"t_lo{i}", [P, 2 * C], F32R) for i in range(2)]
    nmax = [sb(f"nmax{i}", [P, 2, 2]) for i in range(2)]
    p_sb = [sb(f"p_sb{i}", [P, 3 * C]) for i in range(2)]
    pT_sb = [sb(f"pT_sb{i}", [P, 3 * C]) for i in range(2)]
    u_sb = [sb(f"u_sb{i}", [P, TC, H * D]) for i in range(2)]
    wv_raw, wz_raw, wk_raw, wq_raw = (u_sb[j][0:HD, t].rearrange("v (h d) -> v h d", d=D) for j in (1, 0) for t in range(2))
    rsum = [sb(f"rsum{i}", [P, 2, 2]) for i in range(2)]
    rinv = [sb(f"rinv{i}", [P, 2, 2]) for i in range(2)]
    r_sb = [sb(f"r_sb{i}", [P, TC, D]) for i in range(2)]
    stats = [sb(f"stats{i}", [P, TC, 6]) for i in range(2)]
    mv = [sb(f"mv{i}", [P, TC, 2]) for i in range(2)]
    veps = [sb(f"veps{i}", [P, TC]) for i in range(2)]
    rstd = [sb(f"rstd{i}", [P, TC]) for i in range(2)]
    x1_cur = [sb(f"x1_cur{i}", [P, TC, D]) for i in range(2)]
    x1T_sb = sb("x1T_sb", [P, C])
    wg_sb = sb("wg_sb", [P, E])
    lg = sb("lg", [P, GROUPS // 2, E])
    top = sb("top", [P, 2, GROUPS // 2])
    eq = sb("eq", [P, GROUPS // 2, E])
    rank = sb("rank", [P, GROUPS // 2])
    lg2 = sb("lg2", [P, GROUPS // 2, E])
    desc = sb("desc", [P, GROUPS // 2, E])
    desc_i = sb("desc_i", [P, GROUPS // 2, E], I32)
    onehot = sb("onehot", [P, GROUPS // 2, 2, E])
    onehot_b = sb("onehot_b", [P, GROUPS // 2, 2, E], BF16)
    either_b = sb("either_b", [P, GROUPS // 2, E], BF16)
    gap = sb("gap", [P, GROUPS // 2])
    egap = sb("egap", [P, GROUPS // 2])
    egap1 = sb("egap1", [P, GROUPS // 2])
    place = sb("place", [P, GROUPS, E])
    slot_f = sb("slot_f", [P, GROUPS])
    slot_u = sb("slot_u", [P, GROUPS], U32)
    entry = sb("entry", [P, GROUPS, 3], U32)
    entry_step = sb("entry_step", [P, GROUPS, 2], I32)
    blank = keep["w2"][:].rearrange("p e f -> p (e f)")[:, 0:slot_list.shape[0] // P * 3].bitcast(U32).rearrange("p (r w) -> p r w", w=3)
    region_i = sb("region_i", [P, E], I32)
    table = keep["table"]
    TILES = table.shape[2]
    region_f = sb("region_f", [P, E])
    used = sb("used", [P, E])
    used_i = sb("used_i", [P, E], I32)
    tiles_i = sb("tiles_i", [P, E], I32)
    tiles = sb("tiles", [P, E])
    upto = [sb(f"upto{i}", [P, E]) for i in range(2)]
    jump = sb("jump", [P, E])
    tile_i = sb("tile_i", [P, TILES], I32)
    tile_n = sb("tile_n", [P, TILES])
    past, past_j = (w_raw[:].rearrange("p a b -> p (a b)")[:, n * TILES * E:(n + 1) * TILES * E]
                    .rearrange("p (t e) -> p t e", e=E) for n in range(2))
    expert_f = sb("expert_f", [P, TILES])
    row_f = sb("row_f", [P, TILES])
    tri = sb("tri", [P, P], BF16)
    ones_b = sb("ones_b", [P, P], BF16)
    x1_cen = [sb(f"x1_cen{i}", [P, TC, D]) for i in range(2)]
    neghalf = sb("neghalf", [P, TC])
    eps = sb("eps", [P, TC])
    ident = keep["ident"]
    mask = sb("mask", [P, 2 * P])

    S = [ctx.enter_context(nc.psum_tensor(f"psS{i}", [P, 1024], F32)) for i in range(2)]
    T = ctx.enter_context(nc.psum_tensor("psT", [P, 512], F32))
    Z = [ctx.enter_context(nc.psum_tensor(f"psZ{i}", [P, 512], F32)) for i in range(2)]
    M = ctx.enter_context(nc.psum_tensor("psM", [P, 512], F32))

    WQK = [S[n // 2][:, n % 2 * 512:n % 2 * 512 + 512] for n in range(4)]
    WVZ = [T[:], Z[0][:], Z[1][:], M[:]]
    SCORES = [[(h * C, C), (2 * C + h * P, P)] for h in range(2)]
    BLOCKS = [[(2 * C + h * P, h * C, 0, 0), (h * C, h * C + P, 0, 1), (h * C + P, 2 * C + h * P, 1, 1)] for h in range(2)]

    wqk_landed = sem("wqk_landed")
    wvz_landed = sem("wvz_landed")
    wqk_done = sem("wqk_done")
    w_hi_done = sem("w_hi_done")
    w_ready = sem("w_ready")
    consts = sem("consts")
    xt_landed = [sem(f"xt_landed{i}") for i in range(2)]
    xr_landed = [sem(f"xr_landed{i}") for i in range(2)]
    xt_hi_done = sem("xt_hi_done")
    xt_split = sem("xt_split")
    t_done = sem("t_done")
    t_hi_done = sem("t_hi_done")
    t_split = sem("t_split")
    scores_done = sem("scores_done")
    max_done = sem("max_done")
    p_ready = sem("p_ready")
    pT_done = sem("pT_done")
    pT_evac = sem("pT_evac")
    rinv_done = sem("rinv_done")
    p_scaled = sem("p_scaled")
    z_step = sem("z_step")
    wvz_done = sem("wvz_done")
    u_done = sem("u_done")
    u_evac = sem("u_evac")
    r_ready = sem("r_ready")
    bn_done = sem("bn_done")
    stats_done = sem("stats_done")
    veps_done = sem("veps_done")
    rstd_done = sem("rstd_done")
    cen_done = sem("cen_done")
    x1_ready = sem("x1_ready")
    x1T_done = sem("x1T_done")
    x1T_evac = sem("x1T_evac")
    logits_done = sem("logits_done")
    lg_ready = sem("lg_ready")
    wg_landed = sem("wg_landed")
    route_step = sem("route_step")
    onehot_ready = sem("onehot_ready")
    gap_ready = sem("gap_ready")
    egap_ready = sem("egap_ready")
    prefix_done = sem("prefix_done")
    place_ready = sem("place_ready")
    entry_ready = sem("entry_ready")
    entry_next = sem("entry_next")
    table_step = sem("table_step")
    blank_ready = sem("blank_ready")
    lists_written = [sem(f"lists_written{g}") for g in range(GROUPS)]
    route_init = sem("route_init")
    f_landed = [sem(f"f_landed{i}") for i in range(RAW)]
    w2_landed = sem("w2_landed")
    f_hi_done = sem("f_hi_done")
    f_ready = sem("f_ready")
    x1_stored = [sem(f"x1_stored{i}") for i in range(2)]

    block = ctx.enter_context(nc.Block())

    def wait(eng, s, count):
        if not isinstance(count, int) or count > 0:
            eng.wait_ge(s, count)

    w_hi, w_lo, count = keep["w_hi"], keep["w_lo"], keep["count"]
    pieces = [(m, e) for m in range(2) for e in range(E)]
    assert len(pieces) == 2 * NP

    def raw_piece(n):
        n %= RAW
        return w_raw[:, n // 2, (n % 2) * F:(n % 2 + 1) * F]

    class At:

        def __init__(self, i, k, first, last):
            self.i, self.k, self.first, self.last = i, k, first, last
            self.kb, self.hp = k // NP, k % NP

        def pair(self, off):
            return self.i * (2 * NP) + (self.k + off)

        def has(self, off):
            return (not self.first or self.k + off >= 0) and (not self.last or self.k + off < 2 * NP)

        def batch(self, off):
            return self.i * 2 + (self.kb + off)

        def has_batch(self, off):
            return (not self.first or self.kb + off >= 0) and (not self.last or self.kb + off < 2)

        def u_piece(self):
            off = 1 if self.hp >= U_LAG else 0
            if self.has_batch(off):
                return off, (self.hp - U_LAG) % UC
            return None

        def has_route(self, hp):
            return self.k % (2 * NP) == hp and not (self.first and self.k < 2 * NP)

        def trip(self):
            return self.i + (self.k // (2 * NP) - 1)

        def hp_of(self, off):
            return (self.k + off) % NP

        def par(self, off):
            return (self.k + off) % 2

        def bpar(self, off):
            return (self.kb + off) % 2

    def trips(eng, step, tail):
        for k in range(2 * NP):
            step(At(0, k, True, False))
        with eng.Fori(1, TRIPS - 1) as i:
            for k in range(2 * NP):
                step(At(i, k, False, False))
        for k in range(2 * NP + tail):
            step(At(TRIPS - 1, k, False, True))

    DRAIN = 2 * NP
    EARLY_U = [M, Z[0], Z[1]]

    @block.sync
    def _(sp):
        def load_xT(b, j):
            sp.dma_start(xT_raw[j][:], xT[bass.ds(b, 1)].rearrange("b p c -> p (b c)")).then_inc(xt_landed[j], 16)

        load_xT(0, 0)
        for dst, w in ((wk_raw, wk), (wq_raw, wq)):
            sp.dma_start(dst, w).then_inc(wqk_landed, 16)
        for dst, w in ((wv_raw, wv), (wz_raw, wz)):
            sp.dma_start(dst, w).then_inc(wvz_landed, 16)

        def load_x(b, j):
            sp.dma_start(x_res[j][:], x[bass.ds(b, 1)].rearrange("b (t p) d -> p (b t) d", p=P)).then_inc(xr_landed[j], 16)

        def load_piece(n):
            m, e = pieces[n]
            sp.dma_start(raw_piece(n), (w1, w3)[m][e]).then_inc(f_landed[n % RAW], 16)

        def step(at):
            if at.first and at.k + RAW < len(pieces):
                sp.wait_ge(f_ready, at.k + 1)
                load_piece(at.k + RAW)
            if at.hp != 0:
                return
            if at.has_batch(2):
                wait(sp, xt_split, at.batch(1))
                load_xT(at.batch(2), at.bpar(2))
            if at.has_batch(-1):
                wait(sp, x1_ready, at.batch(0))
                sp.dma_start(x1_dram[bass.ds(at.batch(-1), 1)].rearrange("b (t p) d -> p (b t) d", p=P),
                             x1_cur[at.bpar(-1)][:]).then_inc(x1_stored[at.bpar(-1)], 16)
            if at.has_batch(1):
                wait(sp, r_ready, at.batch(0))
                load_x(at.batch(1), at.bpar(1))

        load_x(0, 0)
        load_xT(1, 1)
        sp.dma_start(wg_sb[:], wg).then_inc(wg_landed, 16)
        for n in range(RAW):
            load_piece(n)
        for g in range(GROUPS):
            sp.wait_ge(lists_written[g], 16)
        for e in range(E):
            sp.dma_start(keep["w2"][:, e].rearrange("p (a c) -> p a c", c=D),
                         w2[e].rearrange("(a p) c -> p a c", p=P)).then_inc(w2_landed, 16)
        trips(sp, step, 1 + NP)
        sp.wait_ge(w2_landed, 16 * E)
        for j in range(2):
            sp.wait_ge(x1_stored[j], 16 * TRIPS)

    @block.gpsimd
    def _(pool):
        nc.gpsimd.memset(ident[:], 0.0).then_inc(consts, 1)
        nc.gpsimd.memset(mask[:], 0.0).then_inc(consts, 1)
        nc.gpsimd.memset(tri[:], 1.0).then_inc(consts, 1)
        nc.gpsimd.memset(ones_b[:], 1.0).then_inc(consts, 1)
        nc.gpsimd.memset(neghalf[:], -0.5).then_inc(consts, 1)
        nc.gpsimd.memset(eps[:], EPS).then_inc(consts, 1)
        pool.wait_ge(consts, 6)
        nc.gpsimd.affine_select(out=ident[:], in_=ident[:], compare_op=ALU.not_equal, fill=1.0, base=0,
                                pattern=[[-1, P]], channel_multiplier=1).then_inc(consts, 1)
        nc.gpsimd.affine_select(out=mask[:, P:], in_=mask[:, P:], compare_op=ALU.is_ge, fill=BIG, base=0,
                                pattern=[[-1, P]], channel_multiplier=1).then_inc(consts, 1)

        nc.gpsimd.affine_select(out=tri[:], in_=tri[:], compare_op=ALU.is_gt, fill=0.0, base=0,
                                pattern=[[1, P]], channel_multiplier=-1).then_inc(consts, 1)
        rows = slot_list.shape[0] // P
        nc.gpsimd.memset(blank, 0).then_inc(blank_ready, 1)
        pool.wait_ge(blank_ready, 1)
        nc.gpsimd.iota(blank[:, :, 1], pattern=[[1, rows]], base=2 * N, channel_multiplier=rows).then_inc(blank_ready, 1)
        pool.wait_ge(blank_ready, 2)
        for g in range(GROUPS):
            part = slice(g * rows // GROUPS, (g + 1) * rows // GROUPS)
            pool.dma_start(slot_list.rearrange("(p r) w -> p r w", r=rows)[:, part], blank[:, part]).then_inc(lists_written[g], 16)
        for w, choice in ((0, 0), (1, N)):
            nc.gpsimd.iota(entry[:, :, w].bitcast(I32), pattern=[[P, GROUPS // 2], [choice, 2]], base=-P * GROUPS // 2,
                           channel_multiplier=1).then_inc(route_init, 1)
        nc.gpsimd.iota(entry_step[:], pattern=[[0, GROUPS * 2]], base=P * GROUPS // 2, channel_multiplier=0).then_inc(route_init, 1)
        nc.gpsimd.iota(desc_i[:], pattern=[[0, GROUPS // 2], [-1, E]], base=E, channel_multiplier=0).then_inc(route_init, 1)
        nc.gpsimd.iota(region_i[:], pattern=[[REGION, E]], base=0, channel_multiplier=0).then_inc(route_init, 1)
        nc.gpsimd.iota(tile_i[:], pattern=[[1, TILES]], base=0, channel_multiplier=0).then_inc(route_init, 1)

        def split_piece(n):
            m, e = pieces[n]
            pool.wait_ge(f_hi_done, n + 1)
            nc.gpsimd.tensor_tensor(w_lo[m][:, e], raw_piece(n), w_hi[m][:, e].bitcast(F32), ALU.subtract).then_inc(f_ready, 1)

        def advance(t):
            for g in range(GROUPS):
                pool.wait_ge(lists_written[g], t * 16 + 16)
            places = entry[:, :, 0:2].bitcast(I32)
            nc.gpsimd.tensor_tensor(places, places, entry_step[:], ALU.add).then_inc(entry_next, 1)

        def scatter(t, g):
            wait_alone(pool, consts, (entry_ready, t + 1))
            nc.gpsimd.indirect_dma_start(out=slot_list, out_offset=bass.IndirectOffsetOnAxis(ap=slot_u[:, g:g + 1], axis=0),
                                         in_=entry[:, g], in_offset=None).then_inc(lists_written[g], 16)

        def scale(at):
            n = at.pair(0)
            j = at.par(0)
            pool.wait_ge(rinv_done, n + 1)
            for c, (o, w) in enumerate(SCORES[0]):
                p = p_sb[j][:, o:o + 2 * w].rearrange("p (h k) -> p h k", h=2)
                last = nc.gpsimd.tensor_tensor(p, p, rinv[j][:, :, c:c + 1].to_broadcast([P, 2, w]), ALU.mult)
            last.then_inc(p_scaled, 1)

        def split(b, j, n_trip):
            pool.wait_ge(xt_landed[j], n_trip)
            wait(pool, scores_done, (b - 1) * NP)
            wait(pool, u_done, (b - 1) * UC)
            pool.wait_ge(xt_hi_done, b + 1)
            nc.gpsimd.tensor_tensor(xT_lo[j][:], xT_raw[j][:], xT_hi[j][:].bitcast(F32), ALU.subtract).then_inc(xt_split, 1)

        def step(at):
            if at.hp == 3 and at.has_batch(-1):
                j = at.bpar(-1)
                b = at.batch(-1)
                if not (at.first and at.kb < 3):
                    wait(pool, x1_stored[j], at.i * 16 + ((at.kb - 1) // 2) * 16)
                pool.wait_ge(cen_done, b + 1)
                nc.gpsimd.tensor_tensor(x1_cur[j][:], x1_cen[j][:], rstd[j][:].unsqueeze(2).to_broadcast([P, TC, D]),
                                        ALU.mult).then_inc(x1_ready, 1)
            if at.has(0):
                scale(at)
            if at.first:
                split_piece(at.k)
            if at.has_route(CHOOSE):
                advance(at.trip())
            if at.k % (2 * NP) >= SCATTER and at.has_route(at.k % (2 * NP)):
                scatter(at.trip(), at.k % (2 * NP) - SCATTER)
            if at.hp == NP - 1 and at.has_batch(2):
                split(at.batch(2), at.bpar(2), (at.i + (at.kb + 2) // 2) * 16 + 16)
            if at.hp == 2 and at.has_batch(-1):
                j = at.bpar(-1)
                b = at.batch(-1)
                wait(pool, stats_done, b + 1)
                nc.gpsimd.tensor_tensor(veps[j][:], mv[j][:, :, 1], eps[:], ALU.add).then_inc(veps_done, 1)
                pool.wait_ge(veps_done, b + 1)
                nc.gpsimd.tensor_tensor(rstd[j][:], veps[j][:], neghalf[:], ALU.pow).then_inc(rstd_done, 1)
                pool.wait_ge(rstd_done, b + 1)
                nc.gpsimd.tensor_tensor(x1_cen[j][:], r_sb[j][:], mv[j][:, :, 0:1].to_broadcast([P, TC, D]),
                                        ALU.subtract).then_inc(cen_done, 1)

        split(0, 0, 16)
        split(1, 1, 16)
        trips(pool, step, DRAIN)
        for g in range(GROUPS):
            pool.wait_ge(lists_written[g], TRIPS * 16 + 16)

    @block.scalar
    def _(act):
        def w_high(ready, products, hi, scale):
            act.wait_ge(ready, 1)
            for q, product in enumerate(products):
                nc.scalar.activation(hi[:, q * 512:q * 512 + 512], product, ACT.Copy, scale=scale).then_inc(w_hi_done, 1)

        def t_high(at, off):
            n = at.pair(off)
            act.wait_ge(t_done, n + 1)
            wait(act, scores_done, n - 1)
            nc.scalar.activation(t_hi[at.par(off)][:], T[:], ACT.Copy).then_inc(t_hi_done, 1)

        def xt_high(b, j, n_trip):
            act.wait_ge(xt_landed[j], n_trip)
            wait(act, scores_done, (b - 1) * NP)
            wait(act, u_done, (b - 1) * UC)
            nc.scalar.activation(xT_hi[j][:], xT_raw[j][:], ACT.Copy).then_inc(xt_hi_done, 1)

        def u_copy(b, j, c, bank=M):
            act.wait_ge(u_done, b * UC + (c + 1))
            if c == 0:
                wait(act, z_step, (b - 1) * NP)
            t, quarter = c % 2, c // 2
            nc.scalar.activation(u_sb[j][:, t, quarter * 512:quarter * 512 + 512], bank[:], ACT.Copy).then_inc(u_evac, 1)

        def step(at):
            if at.has(1):
                t_high(at, 1)
            if at.has(0):
                n = at.pair(0)
                j = at.par(0)
                wait(act, pT_done, n - 1)
                wait(act, rinv_done, n - 1)
                for c in range(2):
                    act.wait_ge(max_done, n * 4 + (c * 2 + 2))
                    for h in range(2):
                        o, w = SCORES[h][c]
                        nc.scalar.activation(p_sb[j][:, o:o + w], S[j][:, o:o + w], ACT.Exp, bias=nmax[j][:, h, c:c + 1],
                                             scale=-1.0, accum_out=rsum[j][:, h, c:c + 1]).then_inc(p_ready, 1)
            if at.hp == 4 and at.has_batch(-1):
                act.wait_ge(x1T_done, at.batch(0))
                wait(act, logits_done, at.batch(-1))
                nc.scalar.activation(x1T_sb[:], Z[at.bpar(-1)][:, 0:C], ACT.Copy).then_inc(x1T_evac, 1)
            if at.has_route(CHOOSE):
                act.wait_ge(gap_ready, at.trip() + 1)
                wait(act, entry_ready, at.trip())
                nc.scalar.activation(egap[:], gap[:], ACT.Exp).then_inc(egap_ready, 1)
            if at.hp == NP - 1 and at.has_batch(2):
                xt_high(at.batch(2), at.bpar(2), (at.i + (at.kb + 2) // 2) * 16 + 16)
            if at.u_piece():
                off, c = at.u_piece()
                u_copy(at.batch(off), at.bpar(off), c)
            if at.first:
                n = at.k
                m, e = pieces[n]
                act.wait_ge(f_landed[n % RAW], n // RAW * 16 + 16)
                nc.scalar.activation(w_hi[m][:, e], raw_piece(n), ACT.Copy).then_inc(f_hi_done, 1)

        xt_high(0, 0, 16)
        w_high(wqk_done, WQK, wqk_hi, -SCALE)
        w_high(wvz_done, WVZ, wvz_hi, 1.0 / H)
        t_high(At(0, 0, True, False), 0)
        for c in range(UC - U_LAG):
            u_copy(0, 0, c, EARLY_U[c % 3])
        xt_high(1, 1, 16)
        trips(act, step, DRAIN)

    @block.vector
    def _(dve):
        def w_low(products, hi, lo, scale, before):
            for q, product in enumerate(products):
                cols = slice(q * 512, q * 512 + 512)
                dve.wait_ge(w_hi_done, before + q + 1)
                nc.vector.scalar_tensor_tensor(out=lo[:, cols], in0=product, scalar=scale, in1=hi[:, cols].bitcast(F32),
                                               op0=ALU.mult, op1=ALU.subtract).then_inc(w_ready, 1)

        def t_low(at, off):
            j = at.par(off)
            dve.wait_ge(t_hi_done, at.pair(off + 1))
            nc.vector.tensor_tensor(t_lo[j][:], T[:], t_hi[j][:].bitcast(F32), ALU.subtract).then_inc(t_split, 1)

        w_low(WQK, wqk_hi, wqk_lo, -SCALE, 0)
        w_low(WVZ, wvz_hi, wvz_lo, 1.0 / H, 4)

        def step(at):
            if at.has(0):
                n = at.pair(0)
                j = at.par(0)
                wait_alone(dve, consts, (scores_done, n + 1), (p_ready, (n - 1) * 4))
                for c in range(2):
                    for h in range(2):
                        o, w = SCORES[h][c]
                        s_ap = S[j][:, o:o + w]
                        nc.vector.tensor_tensor_reduce(out=s_ap, in0=s_ap, in1=mask[:, 2 * P - w:], scale=1.0, scalar=3.0e38,
                                                       op0=ALU.add, op1=ALU.min, accum_out=nmax[j][:, h, c:c + 1]).then_inc(max_done, 1)
            if at.has(1):
                t_low(at, 1)
            if at.has(-1):
                n = at.pair(-1)
                j = at.par(-1)
                dve.wait_ge(pT_done, n + 1)
                wait(dve, z_step, n - 1)
                nc.vector.tensor_copy(pT_sb[j][:], S[j][:, 0:3 * C]).then_inc(pT_evac, 1)
            if at.has(0):
                n = at.pair(0)
                j = at.par(0)
                dve.wait_ge(p_ready, n * 4 + 4)
                wait(dve, p_scaled, n - 1)
                nc.vector.reciprocal(rinv[j][:], rsum[j][:]).then_inc(rinv_done, 1)
            if at.hp == 2 and at.has_batch(-1):
                b, j = at.batch(-1), at.bpar(-1)
                dve.wait_ge(z_step, at.batch(0) * NP)
                dve.wait_ge(xr_landed[j], (at.i + (at.kb - 1) // 2) * 16 + 16)
                wait(dve, x1_ready, b - 1)
                nc.vector.tensor_tensor(r_sb[j][:], Z[j][:, 0:TC * D].rearrange("p (t d) -> p t d", t=TC), x_res[j][:],
                                        ALU.add).then_inc(r_ready, 1)
                dve.wait_ge(r_ready, b + 1)
                for t in range(TC):
                    last = nc.vector.bn_stats(stats[j][:, t], r_sb[j][:, t])
                last.then_inc(bn_done, 1)
                wait_alone(dve, consts, (bn_done, b + 1))
                for t in range(TC):
                    last = nc.vector.bn_aggr(mv[j][:, t], stats[j][:, t])
                last.then_inc(stats_done, 1)

            if at.hp == 5 and at.has_batch(-1):
                jt = at.bpar(-1) * TC
                dve.wait_ge(logits_done, at.batch(0))
                nc.vector.tensor_copy(lg[:, jt:jt + TC], Z[at.bpar(-1)][:, 0:TC * E].rearrange("p (t e) -> p t e", e=E)).then_inc(lg_ready, 1)
            if at.has_route(CHOOSE):
                choose(at.trip())
            if at.has_route(ASSIGN):
                assign(at.trip(), Z[at.bpar(0)])

        T4 = GROUPS // 2
        STEPS = 16

        def choose(t):
            n = [0]

            def link(ins):
                n[0] += 1
                ins.then_inc(route_step, 1)
                dve.wait_ge(route_step, t * STEPS + n[0])

            def first_of(values, c):
                link(nc.vector.tensor_reduce(top[:, c], values[:], AX.X, ALU.max))
                link(nc.vector.tensor_tensor(eq[:], values[:], top[:, c].unsqueeze(2).to_broadcast([P, T4, E]), ALU.is_equal))
                link(nc.vector.tensor_tensor(lg2[:] if c else eq[:], eq[:], desc[:], ALU.mult))
                link(nc.vector.tensor_reduce(rank[:], (lg2 if c else eq)[:], AX.X, ALU.max))
                link(nc.vector.tensor_tensor(onehot[:, :, c], (lg2 if c else eq)[:],
                                             rank[:].unsqueeze(2).to_broadcast([P, T4, E]), ALU.is_equal))

            dve.wait_ge(lg_ready, t * 2 + 2)
            wait(dve, place_ready, t)
            first_of(lg, 0)
            link(nc.vector.scalar_tensor_tensor(out=lg2[:], in0=onehot[:, :, 0], scalar=-BIG, in1=lg[:], op0=ALU.mult, op1=ALU.add))
            first_of(lg2, 1)
            nc.vector.tensor_tensor(either_b[:], onehot[:, :, 0], onehot[:, :, 1], ALU.add)
            nc.vector.tensor_copy(onehot_b[:], onehot[:]).then_inc(onehot_ready, 1)
            wait(dve, egap_ready, t)
            nc.vector.tensor_tensor(gap[:], top[:, 1], top[:, 0], ALU.subtract).then_inc(gap_ready, 1)
            assert n[0] == 11

        def assign(t, prefix):
            n = [11]

            def link(ins):
                n[0] += 1
                ins.then_inc(route_step, 1)
                dve.wait_ge(route_step, t * STEPS + n[0])

            counts = prefix[:, 0:(GROUPS + 1) * E].rearrange("p (g e) -> p g e", e=E)
            dve.wait_ge(prefix_done, t + 1)
            dve.wait_ge(entry_next, t + 1)
            link(nc.vector.tensor_tensor(place[:], counts[:, 0:GROUPS], count[:].unsqueeze(1).to_broadcast([P, GROUPS, E]), ALU.add))
            link(nc.vector.tensor_tensor(place[:], place[:], onehot[:].rearrange("p t c e -> p (t c) e"), ALU.mult))
            nc.vector.tensor_tensor(count[:], count[:], counts[:, GROUPS], ALU.add).then_inc(place_ready, 1)
            link(nc.vector.tensor_reduce(slot_f[:], place[:], AX.X, ALU.add))
            nc.vector.tensor_copy(slot_u[:], slot_f[:])
            dve.wait_ge(egap_ready, t + 1)
            link(nc.vector.tensor_scalar(egap1[:], egap[:], 1.0, None, ALU.add))
            w = entry[:].rearrange("p (t c) w -> p t c w", c=2)[:, :, :, 2].bitcast(F32)
            link(nc.vector.reciprocal(w[:, :, 0], egap1[:]))
            nc.vector.tensor_tensor(w[:, :, 1], w[:, :, 0], egap[:], ALU.mult).then_inc(entry_ready, 1)
            assert n[0] == STEPS

        def make_table():
            n = [0]

            def link(ins):
                n[0] += 1
                ins.then_inc(table_step, 1)
                dve.wait_ge(table_step, n[0])

            dve.wait_ge(place_ready, TRIPS)
            dve.wait_ge(f_ready, len(pieces))
            link(nc.vector.tensor_copy(region_f[:], region_i[:]))
            link(nc.vector.tensor_tensor(used[:], count[:], region_f[:], ALU.subtract))
            link(nc.vector.tensor_scalar(used_i[:], used[:], float(P - 1), None, ALU.add))
            link(nc.vector.tensor_scalar(tiles_i[:], used_i[:], P.bit_length() - 1, None, ALU.logical_shift_right))
            link(nc.vector.tensor_copy(tiles[:], tiles_i[:]))
            link(nc.vector.tensor_copy(upto[0][:], tiles[:]))
            for k, d in enumerate((1, 2, 4)):
                a, b = upto[k % 2], upto[(k + 1) % 2]
                nc.vector.tensor_copy(b[:, 0:d], a[:, 0:d])
                link(nc.vector.tensor_tensor(b[:, d:E], a[:, d:E], a[:, 0:E - d], ALU.add))
            total = upto[1]
            link(nc.vector.tensor_scalar(jump[:], tiles[:], -float(P), float(REGION), ALU.mult, ALU.add))
            link(nc.vector.tensor_copy(tile_n[:], tile_i[:]))
            link(nc.vector.tensor_tensor(past[:], tile_n[:].unsqueeze(2).to_broadcast([P, TILES, E]),
                                         total[:].unsqueeze(1).to_broadcast([P, TILES, E]), ALU.is_ge))
            nc.vector.tensor_reduce(expert_f[:], past[:], AX.X, ALU.add)
            link(nc.vector.tensor_tensor(past_j[:], past[:], jump[:].unsqueeze(1).to_broadcast([P, TILES, E]), ALU.mult))
            link(nc.vector.tensor_reduce(row_f[:], past_j[:], AX.X, ALU.add))
            nc.vector.scalar_tensor_tensor(out=table[:, 0], in0=tile_n[:], scalar=float(P), in1=row_f[:], op0=ALU.mult, op1=ALU.add)
            nc.vector.tensor_scalar(table[:, 1], expert_f[:], float(E - 1), None, ALU.min)

        dve.wait_ge(route_init, 6)
        nc.vector.tensor_copy(desc[:], desc_i[:]).then_inc(route_init, 1)
        nc.vector.tensor_copy(count[:], region_i[:]).then_inc(route_init, 1)
        dve.wait_ge(route_init, 8)
        t_low(At(0, 0, True, False), 0)
        trips(dve, step, DRAIN)
        make_table()

    @block.tensor
    def _(pe):
        def project(at, off):
            n = at.pair(off)
            cols = slice(at.hp_of(off) * P, at.hp_of(off) * P + P)
            b_off = (at.k + off) // NP - at.kb
            if at.hp_of(off) == 0:
                pe.wait_ge(xt_split, at.batch(b_off) + 1)
            wait(pe, t_split, n)
            j = at.bpar(b_off)
            for h in range(2):
                out = T[:, h * C:h * C + C]
                cols = slice((2 * at.hp_of(off) + h) * D, (2 * at.hp_of(off) + h + 1) * D)
                nc.tensor.matmul(out, wqk_hi[:, cols], xT_hi[j][:], start=True, stop=False)
                nc.tensor.matmul(out, wqk_hi[:, cols], xT_lo[j][:], start=False, stop=False)
                last = nc.tensor.matmul(out, wqk_lo[:, cols], xT_hi[j][:], start=False, stop=True)
            last.then_inc(t_done, 1)

        def scores(at):
            n = at.pair(0)
            j, jb = at.par(0), at.bpar(0)
            wait(pe, pT_evac, n - 1)
            pe.wait_ge(t_split, n + 1)
            for out, q0, nk in ((S[j][:, 0:2 * C], P, C), (S[j][:, 2 * C:3 * C], 0, P)):
                x_hi, x_lo = (x[jb][:, q0:q0 + P] for x in (xT_hi, xT_lo))
                hi, lo = (t[j][:].rearrange("p (h k) -> p h k", h=2)[:, :, 0:nk] for t in (t_hi, t_lo))
                out = out.rearrange("p (h k) -> p h k", h=2)
                nc.tensor.matmul(out, x_hi, hi, start=True, stop=False)
                nc.tensor.matmul(out, x_hi, lo, start=False, stop=False)
                last = nc.tensor.matmul(out, x_lo, hi, start=False, stop=True)
            last.then_inc(scores_done, 1)

        def transpose_p(at, off):
            n = at.pair(off)
            j = at.par(off)
            pe.wait_ge(p_scaled, n + 1)
            for h in range(2):
                for o, oT, _, _ in BLOCKS[h]:
                    last = nc.tensor.transpose(S[j][:, oT:oT + P], p_sb[j][:, o:o + P], ident[:])
            last.then_inc(pT_done, 1)

        def values(at, off):
            n = at.pair(off)
            j = at.par(off)
            hp = at.hp_of(off)
            b_off = (at.k + off) // NP - at.kb
            b = at.batch(b_off)
            jb = at.bpar(b_off)
            if hp % 2 == 0:
                pe.wait_ge(u_evac, b * UC + (hp + 2))
            if hp == 0:
                wait(pe, r_ready, b - 1)
            pe.wait_ge(pT_evac, n + 1)
            for h in range(2):
                cols = slice((2 * hp + h) * D, (2 * hp + h + 1) * D)
                for _, oT, tk, t in BLOCKS[h]:
                    last = nc.tensor.matmul(Z[jb][:, t * D:t * D + D], pT_sb[j][:, oT:oT + P], u_sb[jb][:, tk, cols], start=(hp == 0 and h == 0 and t == 0),
                                            stop=(hp == NP - 1 and h == 1), skip_group_check=True)
            last.then_inc(z_step, 1)

        def u_chunk(b, j, c, bank=M, banks=1):
            wait(pe, u_evac, b * UC + (c - banks + 1))
            pe.wait_ge(xt_split, b + 1)
            t, quarter = c % 2, c // 2
            cols = slice(quarter * 512, quarter * 512 + 512)
            rows = slice(t * P, t * P + P)
            nc.tensor.matmul(bank[:], xT_hi[j][:, rows], wvz_hi[:, cols], start=True, stop=False)
            nc.tensor.matmul(bank[:], xT_lo[j][:, rows], wvz_hi[:, cols], start=False, stop=False)
            nc.tensor.matmul(bank[:], xT_hi[j][:, rows], wvz_lo[:, cols], start=False, stop=True).then_inc(u_done, 1)

        def step(at):
            if at.has(0):
                scores(at)
            if at.has(1):
                project(at, 1)
            b, hp = at.batch(0), at.hp

            aux = Z[at.bpar(-1)]
            if hp == 4 and at.has_batch(-1):
                pe.wait_ge(x1_ready, b)
                j = at.bpar(-1)
                for t in range(TC):
                    last = nc.tensor.transpose(aux[:, t * P:t * P + P], x1_cur[j][:, t], ident[:])
                last.then_inc(x1T_done, 1)
            if hp == 5 and at.has_batch(-1):
                pe.wait_ge(x1T_evac, b)
                for t in range(TC):
                    last = nc.tensor.matmul(aux[:, t * E:t * E + E], x1T_sb[:, t * P:t * P + P], wg_sb[:], start=True, stop=True)
                last.then_inc(logits_done, 1)
            if at.has_route(ASSIGN):
                pe.wait_ge(onehot_ready, at.trip() + 1)
                aux = Z[at.bpar(0)]
                oh = onehot_b[:].rearrange("p t c e -> p (t c) e")
                nc.tensor.matmul(aux[:, 0:GROUPS * E], tri[:], oh.rearrange("p g e -> p (g e)"), start=True, stop=False,
                                 skip_group_check=True)
                nc.tensor.matmul(aux[:, 0:GROUPS * E].rearrange("p (t c e) -> p t c e", c=2, e=E)[:, :, 1], ones_b[:],
                                 onehot_b[:, :, 0], start=False, stop=False, skip_group_check=True)
                for t in range(GROUPS // 2):
                    after = aux[:, (2 * t + 2) * E:(GROUPS + 1) * E].rearrange("p (g e) -> p g e", e=E)
                    last = nc.tensor.matmul(after, ones_b[:], either_b[:, t:t + 1].to_broadcast([P, GROUPS - 2 * t - 1, E]),
                                            start=False, stop=(t == GROUPS // 2 - 1), skip_group_check=True)
                last.then_inc(prefix_done, 1)
            if at.has(-1):
                transpose_p(at, -1)
            if at.has(-2):
                values(at, -2)
            if at.u_piece():
                off, c = at.u_piece()
                u_chunk(at.batch(off), at.bpar(off), c)

        pe.wait_ge(consts, 9)
        for landed, done, products, left, right in ((wqk_landed, wqk_done, WQK, wk_raw, wq_raw),
                                                    (wvz_landed, wvz_done, WVZ, wv_raw, wz_raw)):
            pe.wait_ge(landed, 32)
            for h in range(H):
                last = nc.tensor.matmul(products[h // 4][:, h % 4 * D:h % 4 * D + D], left[:, h], right[:, h], start=True, stop=True)
            last.then_inc(done, 1)
        pe.wait_ge(wg_landed, 16)
        pe.wait_ge(w_ready, 5)
        project(At(0, 0, True, False), 0)
        pe.wait_ge(w_ready, 8)
        for c in range(UC - U_LAG):
            u_chunk(0, 0, c, EARLY_U[c % 3], 3)
        trips(pe, step, DRAIN)


def experts_phase(nc, ctx, keep, x1, slot_list, y, x1_all):
    w1_hi, w3_hi = keep["w_hi"]
    w1_lo, w3_lo = keep["w_lo"]
    w2 = keep["w2"]
    table, ident = keep["table"], keep["ident"]
    E, F = w1_hi.shape[1:]
    N = x1.shape[0] * x1.shape[1]
    D = x1.shape[2]
    A = F // P
    REGION = N
    RING = 8
    LAG = 5
    TILES = table.shape[2]
    TRIP = 3 * RING
    TRIPS = (TILES + RING) // TRIP
    assert TRIPS * TRIP == TILES + RING

    def sb(name, shape, dt=F32):
        return ctx.enter_context(nc.sbuf_tensor(name, shape, dt))

    def ps(name):
        return ctx.enter_context(nc.psum_tensor(name, [P, 512], F32))

    def sem(name):
        return ctx.enter_context(nc.semaphore(name))

    entry = [sb(f"slots{i}", [P, 3], U32) for i in range(RING)]
    xg = [sb(f"xg{i}", [P, D]) for i in range(RING)]
    xg_hi = [sb(f"xg_hi{i}", [P, P], F32R) for i in range(RING)]
    xg_lo = [sb(f"xg_lo{i}", [P, P], F32R) for i in range(RING)]
    gate = [sb(f"gate{i}", [P, F]) for i in range(2)]
    hid = [sb(f"hid{i}", [P, F]) for i in range(2)]
    hidT_sb = [sb(f"hidT_sb{i}", [P, F]) for i in range(2)]
    y_sb = [sb(f"y_sb{i}", [P, D]) for i in range(RING)]
    H1 = [ps(f"psH1{i}") for i in range(2)]
    H3 = [ps(f"psH3{i}") for i in range(2)]
    XT, HT, YO = ps("psXT"), ps("psHT"), ps("psYO")

    one = sb("one", [P, 1])
    one_silu = sb("one_silu", [P, 1])
    consts = sem("consts2")
    silu_loaded = sem("silu_loaded")
    x1_landed = sem("x1_landed")
    slots_landed = [sem(f"slots_landed{i}") for i in range(RING)]
    x_gathered = [sem(f"x_gathered{i}") for i in range(RING)]
    xT_done = sem("xT_done")
    xT_hi_done = sem("xT_hi_done")
    xT_split = sem("xT_split")
    up_done = sem("up_done")
    gate_done = sem("gate_done")
    hid_ready = sem("hid_ready")
    hidT_done = sem("hidT_done")
    hidT_evac = sem("hidT_evac")
    down_done = sem("down_done")
    y_ready = sem("y_ready")
    y_stored = [sem(f"y_stored{i}") for i in range(RING)]

    block = ctx.enter_context(nc.Block())

    def wait(eng, s, value):
        if not isinstance(value, int) or value > 0:
            eng.wait_ge(s, value)

    class At:

        def __init__(self, i, k, first, last):
            self.i, self.k, self.first, self.last = i, k, first, last

        def tile(self, off):
            return self.i * TRIP + (self.k + off - RING)

        def has(self, off):
            return (not self.first or self.k + off >= RING) and (not self.last or self.k + off < TRIP)

        def ring(self, off, n=RING):
            return (self.k + off) % n

        def use(self, off):
            return self.i * (TRIP // RING) + ((self.k + off) // RING - 1)

    def trips(eng, step, tail=RING):
        for k in range(RING, TRIP):
            step(At(0, k, True, False))
        for k in range(TRIP):
            step(At(1, k, False, False))
        with eng.Fori(2, TRIPS - 1) as i:
            for k in range(TRIP):
                step(At(i, k, False, False))
        for k in range(TRIP + tail):
            step(At(TRIPS - 1, k, False, True))

    @block.sync
    def _(sp):
        def load_slots(at, off):
            r = at.ring(off)
            wait(sp, y_stored[r], at.use(off) * 16)
            row = sp.value_load(table[0:1, 0, bass.ds(at.tile(off), 1)], min_val=0, max_val=E * (REGION + P) - P)
            sp.dma_start(entry[r][:], slot_list[bass.ds(row, P)]).then_inc(slots_landed[r], 16)

        trips(sp, lambda at: at.has(0) and load_slots(at, 0), 0)
        x1_tiles = x1.rearrange("b (t p) d -> p (b t) d", p=P)
        quarter = N // P // 4
        for n in range(4):
            part = slice(n * quarter, (n + 1) * quarter)
            sp.dma_start(x1_all[:, part], x1_tiles[:, part]).then_inc(x1_landed, 16)
        sp.wait_ge(x1_landed, 16 * 4)

    @block.gpsimd
    def _(pool):
        nc.gpsimd.memset(one[:], 1.0).then_inc(consts, 1)
        pool.wait_ge(consts, 1)

        def step(at):
            if at.has(-LAG):
                r = at.ring(-LAG)
                wait_alone(pool, consts, (y_ready, at.tile(1 - LAG)))
                nc.gpsimd.indirect_dma_start(out=y, out_offset=bass.IndirectOffsetOnAxis(ap=entry[r][:, 1:2], axis=0),
                                             in_=y_sb[r][:], in_offset=None).then_inc(y_stored[r], 16)
            if at.has(0):
                r = at.ring(0)
                wait_alone(pool, consts, (slots_landed[r], at.use(0) * 16 + 16), (xT_done, at.tile(0) - RING + 1))
                nc.gpsimd.indirect_dma_start(out=xg[r][:], out_offset=None, in_=x1.rearrange("b c d -> (b c) d"),
                                             in_offset=bass.IndirectOffsetOnAxis(ap=entry[r][:, 0:1], axis=0)
                                             ).then_inc(x_gathered[r], 16)

        trips(pool, step)
        for r in range(RING):
            pool.wait_ge(y_stored[r], TILES // RING * 16)

    @block.scalar
    def _(act):
        def x_high(at, off):
            act.wait_ge(xT_done, at.tile(off + 1))
            wait(act, up_done, at.tile(off) - RING + 1)
            nc.scalar.activation(xg_hi[at.ring(off)][:], XT[:, 0:P], ACT.Copy).then_inc(xT_hi_done, 1)

        def step(at):
            if at.has(1):
                x_high(at, 1)
            if at.has(0):
                j = at.ring(0, 2)
                act.wait_ge(up_done, at.tile(1))
                wait(act, hid_ready, at.tile(-1))
                nc.scalar.activation(gate[j][:], H1[j][:], ACT.Silu).then_inc(gate_done, 1)
            if at.has(-2):
                act.wait_ge(down_done, at.tile(-1))
                r = at.ring(-2)
                wait(act, y_stored[r], at.use(-2) * 16)
                nc.scalar.activation(y_sb[r][:], YO[:, 0:D], ACT.Copy, scale=entry[r][:, 2:3].bitcast(F32)).then_inc(y_ready, 1)
            if at.has(-1):
                j = at.ring(-1, 2)
                act.wait_ge(hidT_done, at.tile(0))
                wait(act, down_done, at.tile(-2))
                nc.scalar.activation(hidT_sb[j][:], HT[:], ACT.Copy).then_inc(hidT_evac, 1)

        act.wait_ge(consts, 1)
        nc.scalar.activation(one_silu[:], one[:], ACT.Silu).then_inc(silu_loaded, 1)
        x_high(At(0, RING, True, False), 0)
        trips(act, step)

    @block.vector
    def _(dve):
        def x_low(at, off):
            r = at.ring(off)
            dve.wait_ge(xT_hi_done, at.tile(off + 1))
            nc.vector.tensor_tensor(xg_lo[r][:], XT[:, 0:P], xg_hi[r][:].bitcast(F32), ALU.subtract).then_inc(xT_split, 1)

        def step(at):
            if at.has(1):
                x_low(at, 1)
            if at.has(0):
                j = at.ring(0, 2)
                dve.wait_ge(gate_done, at.tile(1))
                wait(dve, hidT_done, at.tile(-1))
                nc.vector.tensor_tensor(hid[j][:], H3[j][:], gate[j][:], ALU.mult).then_inc(hid_ready, 1)
        x_low(At(0, RING, True, False), 0)
        trips(dve, step)

    @block.tensor
    def _(pe):
        def transpose_x(at, off):
            r = at.ring(off)
            pe.wait_ge(x_gathered[r], at.use(off) * 16 + 16)
            wait(pe, xT_split, at.tile(off))
            nc.tensor.transpose(XT[:, 0:P], xg[r][:], ident[:]).then_inc(xT_done, 1)

        def expert(at, off):
            return pe.value_load(table[0:1, 1, bass.ds(at.tile(off), 1)], min_val=0, max_val=E - 1)

        def up(at, e):
            j, r = at.ring(0, 2), at.ring(0)
            e = bass.ds(e, 1)
            pe.wait_ge(xT_split, at.tile(1))
            wait(pe, hid_ready, at.tile(-1))
            for out, hi, lo in ((H1[j], w1_hi, w1_lo), (H3[j], w3_hi, w3_lo)):
                w_h, w_l = (w[:, e].rearrange("p e f -> p (e f)") for w in (hi, lo))
                nc.tensor.matmul(out[:], xg_hi[r][:], w_h, start=True, stop=False)
                nc.tensor.matmul(out[:], xg_lo[r][:], w_h, start=False, stop=False)
                last = nc.tensor.matmul(out[:], xg_hi[r][:], w_l, start=False, stop=True)
            last.then_inc(up_done, 1)

        def transpose_hid(at, off):
            j = at.ring(off, 2)
            pe.wait_ge(hid_ready, at.tile(off + 1))
            wait(pe, hidT_evac, at.tile(off))
            for a in range(A):
                last = nc.tensor.transpose(HT[:, a * P:a * P + P], hid[j][:, a * P:a * P + P], ident[:])
            last.then_inc(hidT_done, 1)

        def down(at, off, e):
            j = at.ring(off, 2)
            e = bass.ds(e, 1)
            pe.wait_ge(hidT_evac, at.tile(off + 1))
            wait(pe, y_ready, at.tile(off))
            w = w2[:, e].rearrange("p e f -> p (e f)")
            for a in range(A):
                last = nc.tensor.matmul(YO[:, 0:D], hidT_sb[j][:, a * P:a * P + P], w[:, a * D:a * D + D],
                                        start=(a == 0), stop=(a == A - 1))
            last.then_inc(down_done, 1)

        experts = {}

        def step(at):
            if at.k == 0:
                experts.clear()
                for off in (-2, -1, 0):
                    if at.has(off):
                        experts[off] = expert(at, off)
            if at.has(0):
                up(at, experts[at.k])
            if at.has(1) and at.k + 1 < TRIP:
                experts[at.k + 1] = expert(at, 1)
            if at.has(1):
                transpose_x(at, 1)
            if at.has(-2):
                down(at, -2, experts[at.k - 2])
            if at.has(-1):
                transpose_hid(at, -1)

        transpose_x(At(0, RING, True, False), 0)
        experts[RING] = expert(At(0, RING, True, False), 0)
        trips(pe, step)


def finish_phase(nc, ctx, x1_all, y, out):
    NB, C, D = out.shape
    N = NB * C
    TB = 8
    STEPS = N // (P * TB)

    def sb(name, shape, dt=F32):
        return ctx.enter_context(nc.sbuf_tensor(name, shape, dt))

    def sem(name):
        return ctx.enter_context(nc.semaphore(name))

    R = 4
    ya = [sb(f"ya{i}", [P, TB, D]) for i in range(R)]
    yb = [sb(f"yb{i}", [P, TB, D]) for i in range(R)]
    s1 = [sb(f"s1{i}", [P, TB, D]) for i in range(R)]
    s2 = [sb(f"s2{i}", [P, TB, D]) for i in range(R)]
    st = [sb(f"st{i}", [P, TB, 6]) for i in range(R)]
    mv = [sb(f"mv2{i}", [P, TB, 2]) for i in range(R)]
    ve = [sb(f"ve{i}", [P, TB]) for i in range(R)]
    rs = [sb(f"rs{i}", [P, TB]) for i in range(R)]
    nm = [sb(f"nm{i}", [P, TB]) for i in range(R)]
    o = [sb(f"o{i}", [P, TB, D]) for i in range(R)]
    neghalf = sb("neghalf2", [P, TB])
    eps = sb("eps2", [P, TB])
    consts = sem("consts3")
    landed = [sem(f"landed{i}") for i in range(R)]
    sum1 = sem("sum1")
    sum2 = sem("sum2")
    st_done = sem("st_done")
    mv_done = sem("mv_done")
    ve_done = sem("ve_done")
    rs_done = sem("rs_done")
    o_ready = sem("o_ready")
    nm_done = sem("nm_done")
    stored = [sem(f"stored{i}") for i in range(R)]
    block = ctx.enter_context(nc.Block())

    def rows(a, n):
        return a[n * P * TB:(n + 1) * P * TB].rearrange("(t p) d -> p t d", p=P)

    of = out.rearrange("b c d -> (b c) d")

    @block.sync
    def _(sp):
        for n in range(STEPS):
            r = n % R
            if n >= R:
                sp.wait_ge(sum2, n - R + 1)
            sp.dma_start(ya[r][:], rows(y, n)).then_inc(landed[r], 16)
            sp.dma_start(yb[r][:], rows(y[N:2 * N], n)).then_inc(landed[r], 16)

    @block.vector
    def _(dve):
        def shift(n):
            r = n % R
            dve.wait_ge(rs_done, n + 1)
            nc.vector.scalar_tensor_tensor(out=nm[r][:], in0=mv[r][:, :, 0], scalar=-1.0, in1=rs[r][:], op0=ALU.mult,
                                           op1=ALU.mult).then_inc(nm_done, 1)

        for n in range(STEPS):
            r = n % R
            dve.wait_ge(sum1, n + 1)
            if n >= R:
                dve.wait_ge(o_ready, n - R + 1)
            nc.vector.tensor_tensor(s2[r][:], s1[r][:], yb[r][:], ALU.add).then_inc(sum2, 1)
            dve.wait_ge(sum2, n + 1)
            for t in range(TB):
                last = nc.vector.bn_stats(st[r][:, t], s2[r][:, t])
            last.then_inc(st_done, 1)
            dve.wait_ge(st_done, n + 1)
            for t in range(TB):
                last = nc.vector.bn_aggr(mv[r][:, t], st[r][:, t])
            last.then_inc(mv_done, 1)
            if n:
                shift(n - 1)
        shift(STEPS - 1)

    @block.gpsimd
    def _(pool):
        nc.gpsimd.memset(neghalf[:], -0.5).then_inc(consts, 1)
        nc.gpsimd.memset(eps[:], EPS).then_inc(consts, 1)
        pool.wait_ge(consts, 2)

        def first_sum(n):
            r = n % R
            pool.wait_ge(landed[r], n // R * 32 + 32)
            if n >= R:
                pool.wait_ge(sum2, n - R + 1)
            nc.gpsimd.tensor_tensor(s1[r][:], x1_all[:, n * TB:(n + 1) * TB], ya[r][:], ALU.add).then_inc(sum1, 1)

        first_sum(0)
        for n in range(STEPS):
            r = n % R
            if n + 1 < STEPS:
                first_sum(n + 1)
            pool.wait_ge(mv_done, n + 1)
            nc.gpsimd.tensor_tensor(ve[r][:], mv[r][:, :, 1], eps[:], ALU.add).then_inc(ve_done, 1)
            pool.wait_ge(ve_done, n + 1)
            nc.gpsimd.tensor_tensor(rs[r][:], ve[r][:], neghalf[:], ALU.pow).then_inc(rs_done, 1)

    @block.scalar
    def _(act):
        for n in range(STEPS):
            r = n % R
            act.wait_ge(nm_done, n + 1)
            if n >= R:
                act.wait_ge(stored[r], n // R * 16)
            for t in range(TB):
                last = nc.scalar.activation(o[r][:, t], s2[r][:, t], ACT.Identity, bias=nm[r][:, t:t + 1], scale=rs[r][:, t:t + 1])
            last.then_inc(o_ready, 1)
            act.wait_ge(o_ready, n + 1)
            act.dma_start(rows(of, n), o[r][:]).then_inc(stored[r], 16)
        for r in range(R):
            act.wait_ge(stored[r], (STEPS - 1 - r) // R * 16 + 16)


def program(nc, xT, x, wq, wk, wv, wz, wg, w1, w3, w2, out):
    NB, C, D = x.shape
    N = NB * C
    E, _, F = w1.shape
    x1 = nc.dram_tensor("x1", [NB, C, D], F32).ap()
    slot_list = nc.dram_tensor("slot_list", [E * (N + P), 3], U32).ap()
    y = nc.dram_tensor("y", [2 * N + E * (N + P), D], F32).ap()
    with ExitStack() as ctx:
        def sb(name, shape, dt=F32):
            return ctx.enter_context(nc.sbuf_tensor(name, shape, dt))

        keep = {
            "w_hi": [sb(f"f{n}_hi", [P, E, F], F32R) for n in range(2)],
            "w_lo": [sb(f"f{n}_lo", [P, E, F], F32R) for n in range(2)],
            "w2": sb("f2", [P, E, F]),
            "count": sb("count", [P, E]),
            "ident": sb("ident", [P, P]),
            "table": sb("table", [P, 2, 2 * N // P + E], I32),
        }
        with ExitStack() as inner:
            attention_phase(nc, inner, keep, xT, x, wq, wk, wv, wz, wg, w1, w3, w2, x1, slot_list)
        x1_all = sb("x1_all", [P, N // P, D])
        with ExitStack() as inner:
            experts_phase(nc, inner, keep, x1, slot_list, y, x1_all)
        with ExitStack() as inner:
            finish_phase(nc, inner, x1_all, y, out)


def kernel(**inputs):
    import numpy as _np
    import concourse.bacc as _bacc
    from concourse import mybir as _mybir
    from concourse.bass_utils import run_bass_kernel_spmd as _run

    x = _np.asarray(inputs["L0_attn_x"])
    lay = {
        "xT": x.transpose(0, 2, 1),
        "x": x,
        "wq": _np.asarray(inputs["L0_attn_Q"]).transpose(0, 2, 1),
        "wk": _np.asarray(inputs["L0_attn_K"]).transpose(0, 2, 1),
        "wv": _np.asarray(inputs["L0_attn_V"]).transpose(0, 2, 1),
        "wz": _np.asarray(inputs["L0_attn_W"]).transpose(1, 2, 0),
        "wg": _np.asarray(inputs["L0_ffn_Wg"]),
        "w1": _np.asarray(inputs["L0_ffn_W1"]),
        "w3": _np.asarray(inputs["L0_ffn_W3"]),
        "w2": _np.asarray(inputs["L0_ffn_W2"]),
    }
    nc = _bacc.Bacc("TRN2", target_bir_lowering=False, num_devices=1)
    arrays, args = {}, []
    for name, a in lay.items():
        a = _np.ascontiguousarray(a)
        arrays[f"in_{name}"] = a
        args.append(nc.dram_tensor(f"in_{name}", a.shape, _mybir.dt.from_np(a.dtype), kind="ExternalInput").ap())
    out = nc.dram_tensor("out_0", x.shape, _mybir.dt.float32, kind="ExternalOutput").ap()
    program(nc, *args, out)
    r = _run(nc, [arrays], core_ids=[0])
    return r.results[0]["out_0"]
```
